# Optimizing a Trainium2 kernel written in Bass

```python
import numpy as np
import jax
import jax.numpy as jnp

def _softmax(x, axis=-1):
    return jax.nn.softmax(x, axis=axis)

def _gelu(x):
    return jax.nn.gelu(x, approximate=True)

def _silu(x):
    return jax.nn.silu(x)

def _sigmoid(x):
    return jax.nn.sigmoid(x)

def _layernorm(x, axis=-1, eps=1e-05):
    m = jnp.mean(x, axis=axis, keepdims=True)
    v = jnp.var(x, axis=axis, keepdims=True)
    return (x - m) / jnp.sqrt(v + eps)

def _scatter_add(tgt, idx, src, axis=0):
    return tgt.at[idx].add(src)

def _segment_sum(src, seg, n):
    return jax.ops.segment_sum(src, seg, n)
kernel_name = 'mk_seq_preln_d2_jaxref_r8_0a0efd'

def setup_inputs(seed: int=0):
    np.random.seed(seed)
    _w = jnp.asarray

    def _L0_attn_setup():
        import jax, jax.numpy as jnp
        import numpy as np
        D_MODEL = 128
        NHEAD = 16
        HEAD_DIM = D_MODEL // NHEAD
        SCALE = float(np.sqrt(HEAD_DIM))
        key = jax.random.key(seed)
        ks = jax.random.split(key, 6)
        B, T = (2, 256)
        x = jax.random.normal(ks[0], (B, T, D_MODEL), dtype=jnp.float32)
        s = 1.0 / np.sqrt(D_MODEL)
        qkv_w = jax.random.uniform(ks[1], (3 * D_MODEL, D_MODEL), jnp.float32, -s, s)
        qkv_b = jax.random.uniform(ks[2], (3 * D_MODEL,), jnp.float32, -s, s)
        out_w = jax.random.uniform(ks[3], (D_MODEL, D_MODEL), jnp.float32, -s, s)
        out_b = jax.random.uniform(ks[4], (D_MODEL,), jnp.float32, -s, s)
        decay_alpha = jnp.full((NHEAD,), 0.1, dtype=jnp.float32)
        return {'x': x, 'qkv_w': qkv_w, 'qkv_b': qkv_b, 'out_w': out_w, 'out_b': out_b, 'decay_alpha': decay_alpha}
    _L0_attn_in = _L0_attn_setup()

    def _L0_ffn_setup():
        import jax, jax.numpy as jnp
        import numpy as np
        D_MODEL = 128
        key = jax.random.key(seed)
        k_x, k_w, k_a1, k_a2 = jax.random.split(key, 4)
        x = jax.random.normal(k_x, (4, 256, D_MODEL), dtype=jnp.float32)
        weight = jax.random.normal(k_w, (D_MODEL, D_MODEL), dtype=jnp.float32) * 0.02
        aux_weight1 = jax.random.normal(k_a1, (D_MODEL, D_MODEL), dtype=jnp.float32) * 0.02
        aux_weight2 = jax.random.normal(k_a2, (D_MODEL, D_MODEL), dtype=jnp.float32) * 0.02
        bias = jnp.zeros((D_MODEL,), dtype=jnp.float32)
        return {'x': x, 'weight': weight, 'aux_weight1': aux_weight1, 'aux_weight2': aux_weight2, 'bias': bias}
    _L0_ffn_in = _L0_ffn_setup()

    def _L1_attn_setup():
        import jax, jax.numpy as jnp
        import numpy as np
        import math
        B, S, D = (4, 256, 128)
        H = 16
        HD = D // H
        DL = 32
        LAMBDA_DECAY = 0.01
        key = jax.random.key(seed)
        ks = jax.random.split(key, 8)
        sc = lambda fan_in: 1.0 / math.sqrt(fan_in)
        return {'x': jax.random.normal(ks[0], (B, S, D), dtype=jnp.float32), 'W_q': jax.random.normal(ks[1], (D, D), dtype=jnp.float32) * sc(D), 'W_k': jax.random.normal(ks[2], (D, D), dtype=jnp.float32) * sc(D), 'W_v': jax.random.normal(ks[3], (D, D), dtype=jnp.float32) * sc(D), 'W_o': jax.random.normal(ks[4], (D, D), dtype=jnp.float32) * sc(D), 'W_down_kv': jax.random.normal(ks[5], (D, DL), dtype=jnp.float32) * sc(D), 'W_up_k': jax.random.normal(ks[6], (DL, D), dtype=jnp.float32) * sc(DL), 'W_up_v': jax.random.normal(ks[7], (DL, D), dtype=jnp.float32) * sc(DL)}
    _L1_attn_in = _L1_attn_setup()

    def _L1_ffn_setup():
        import jax, jax.numpy as jnp
        import numpy as np
        import math
        D_IN = 128
        FEATURES = (512, 512, 128)
        BATCH, SEQ = (8, 256)

        def _conn_dense(kernel_bool, x):
            w = jnp.where(kernel_bool, jnp.float32(1.0), jnp.float32(-1.0))
            return x @ w
        key = jax.random.key(seed)
        kx, kk0, kk1, kk2 = jax.random.split(key, 4)
        x = jax.random.normal(kx, (BATCH, SEQ, D_IN), dtype=jnp.float32)
        k0 = jax.random.randint(kk0, (2 * D_IN, FEATURES[0]), 0, 2).astype(jnp.bool_)
        k1 = jax.random.randint(kk1, (FEATURES[0], FEATURES[1]), 0, 2).astype(jnp.bool_)
        k2 = jax.random.randint(kk2, (FEATURES[1], FEATURES[2]), 0, 2).astype(jnp.bool_)
        s0 = jnp.asarray(1.0 / math.sqrt(2 * D_IN), dtype=jnp.float32)
        s1 = jnp.asarray(1.0 / math.sqrt(FEATURES[0]), dtype=jnp.float32)
        s2 = jnp.asarray(1.0 / math.sqrt(FEATURES[1]), dtype=jnp.float32)
        return {'x': x, 'k0': k0, 'k1': k1, 'k2': k2, 's0': s0, 's1': s1, 's2': s2}
    _L1_ffn_in = _L1_ffn_setup()
    _d = {'L0_attn_x': _L0_attn_in['x'], 'L0_attn_qkv_w': _L0_attn_in['qkv_w'], 'L0_attn_qkv_b': _L0_attn_in['qkv_b'], 'L0_attn_out_w': _L0_attn_in['out_w'], 'L0_attn_out_b': _L0_attn_in['out_b'], 'L0_attn_decay_alpha': _L0_attn_in['decay_alpha'], 'L0_ffn_weight': _L0_ffn_in['weight'], 'L0_ffn_aux_weight1': _L0_ffn_in['aux_weight1'], 'L0_ffn_aux_weight2': _L0_ffn_in['aux_weight2'], 'L0_ffn_bias': _L0_ffn_in['bias'], 'L1_attn_W_q': _L1_attn_in['W_q'], 'L1_attn_W_k': _L1_attn_in['W_k'], 'L1_attn_W_v': _L1_attn_in['W_v'], 'L1_attn_W_o': _L1_attn_in['W_o'], 'L1_attn_W_down_kv': _L1_attn_in['W_down_kv'], 'L1_attn_W_up_k': _L1_attn_in['W_up_k'], 'L1_attn_W_up_v': _L1_attn_in['W_up_v'], 'L1_ffn_k0': _L1_ffn_in['k0'], 'L1_ffn_k1': _L1_ffn_in['k1'], 'L1_ffn_k2': _L1_ffn_in['k2'], 'L1_ffn_s0': _L1_ffn_in['s0'], 'L1_ffn_s1': _L1_ffn_in['s1'], 'L1_ffn_s2': _L1_ffn_in['s2']}
    _x0 = _d['L0_attn_x']
    _d['L0_attn_x'] = jax.random.normal(jax.random.fold_in(jax.random.key(seed), 1), (8, 256, 128), dtype=_x0.dtype)
    del _x0
    return _d

def reference(L0_attn_x, L0_attn_qkv_w, L0_attn_qkv_b, L0_attn_out_w, L0_attn_out_b, L0_attn_decay_alpha, L0_ffn_weight, L0_ffn_aux_weight1, L0_ffn_aux_weight2, L0_ffn_bias, L1_attn_W_q, L1_attn_W_k, L1_attn_W_v, L1_attn_W_o, L1_attn_W_down_kv, L1_attn_W_up_k, L1_attn_W_up_v, L1_ffn_k0, L1_ffn_k1, L1_ffn_k2, L1_ffn_s0, L1_ffn_s1, L1_ffn_s2):

    def _L0_attn_ref(x, qkv_w, qkv_b, out_w, out_b, decay_alpha):
        import jax, jax.numpy as jnp
        import numpy as np
        D_MODEL = 128
        NHEAD = 16
        HEAD_DIM = D_MODEL // NHEAD
        SCALE = float(np.sqrt(HEAD_DIM))
        B, T, D = x.shape
        qkv = x @ qkv_w.T + qkv_b
        qkv = qkv.reshape(B, T, 3, NHEAD, HEAD_DIM).transpose(2, 0, 3, 1, 4)
        q, k, v = (qkv[0], qkv[1], qkv[2])
        logits = jnp.einsum('bhqd,bhkd->bhqk', q, k) / SCALE
        pos = jnp.arange(T, dtype=jnp.float32)
        dist = jnp.abs(pos[None, :] - pos[:, None])
        alpha = jax.nn.softplus(decay_alpha)
        logits = logits - alpha[:, None, None] * dist[None]
        attn = jax.nn.softmax(logits, axis=-1)
        out = jnp.einsum('bhqk,bhkd->bhqd', attn, v)
        out = out.transpose(0, 2, 1, 3).reshape(B, T, D)
        out = out @ out_w.T + out_b
        return out

    def _L0_ffn_ref(x, weight, aux_weight1, aux_weight2, bias):
        import jax, jax.numpy as jnp
        import numpy as np
        D_MODEL = 128
        h = jnp.einsum('btc,cd->btd', x, weight)
        h = jnp.einsum('btc,cd->btd', h, aux_weight1)
        h = jnp.einsum('btc,cd->btd', h, aux_weight2)
        return jnp.tanh(h + bias)

    def _L1_attn_ref(x, W_q, W_k, W_v, W_o, W_down_kv, W_up_k, W_up_v):
        import jax, jax.numpy as jnp
        import numpy as np
        import math
        B, S, D = (4, 256, 128)
        H = 16
        HD = D // H
        DL = 32
        LAMBDA_DECAY = 0.01
        b, s, d = x.shape
        q = x @ W_q
        k = x @ W_k
        v = x @ W_v
        latent_kv = (k + v) @ W_down_kv
        k_rec = (latent_kv @ W_up_k).reshape(b, s, H, HD).transpose(0, 2, 1, 3)
        v_rec = (latent_kv @ W_up_v).reshape(b, s, H, HD).transpose(0, 2, 1, 3)
        qh = q.reshape(b, s, H, HD).transpose(0, 2, 1, 3)
        scores = jnp.einsum('bhqd,bhkd->bhqk', qh, k_rec) / math.sqrt(d)
        t = jnp.arange(s, dtype=jnp.float32)
        decay = jnp.exp(-LAMBDA_DECAY * jnp.abs(t[:, None] - t[None, :]))
        scores = scores * decay[None, None, :, :]
        attn = jax.nn.softmax(scores, axis=-1)
        out = jnp.einsum('bhqk,bhkd->bhqd', attn, v_rec)
        out = out.transpose(0, 2, 1, 3).reshape(b, s, d)
        return out @ W_o

    def _L1_ffn_ref(x, k0, k1, k2, s0, s1, s2):
        import jax, jax.numpy as jnp
        import numpy as np
        import math
        D_IN = 128
        FEATURES = (512, 512, 128)
        BATCH, SEQ = (8, 256)

        def _conn_dense(kernel_bool, x):
            w = jnp.where(kernel_bool, jnp.float32(1.0), jnp.float32(-1.0))
            return x @ w
        h = jnp.concatenate([x, -x], axis=-1)
        h = s0 * _conn_dense(k0, h)
        h = jax.nn.relu(h) * 2
        h = s1 * _conn_dense(k1, h)
        h = jax.nn.relu(h) * 2
        h = s2 * _conn_dense(k2, h)
        return h
    x = L0_attn_x
    x = x + _L0_attn_ref(_layernorm(x, axis=-1), L0_attn_qkv_w, L0_attn_qkv_b, L0_attn_out_w, L0_attn_out_b, L0_attn_decay_alpha)
    x = x + _L0_ffn_ref(_layernorm(x, axis=-1), L0_ffn_weight, L0_ffn_aux_weight1, L0_ffn_aux_weight2, L0_ffn_bias)
    x = x + _L1_attn_ref(_layernorm(x, axis=-1), L1_attn_W_q, L1_attn_W_k, L1_attn_W_v, L1_attn_W_o, L1_attn_W_down_kv, L1_attn_W_up_k, L1_attn_W_up_v)
    x = x + _L1_ffn_ref(_layernorm(x, axis=-1), L1_ffn_k0, L1_ffn_k1, L1_ffn_k2, L1_ffn_s0, L1_ffn_s1, L1_ffn_s2)
    return x

_drawn_inputs = setup_inputs


def setup_inputs(seed=0):
    import zlib

    import numpy as np

    out = dict(_drawn_inputs(seed))
    spreads = {'L0_attn_decay_alpha': (0.10000000149011612, 0.6), 'L0_ffn_bias': (0.0, 0.1)}
    factors = {'L0_ffn_weight': 4.954, 'L0_ffn_aux_weight1': 4.862, 'L0_ffn_aux_weight2': 4.932}
    for name, (base, spread) in spreads.items():
        noise = np.random.default_rng([zlib.crc32(name.encode()), seed]).standard_normal(out[name].shape)
        drawn = base * np.exp(spread * noise) if base else spread * noise
        out[name] = jnp.asarray(drawn.astype(out[name].dtype))
    for name, factor in factors.items():
        out[name] = (out[name] * factor).astype(out[name].dtype)
    return out
```

```python
from contextlib import ExitStack

import concourse.bass as bass
from concourse import mybir

F32 = mybir.dt.float32
F16 = mybir.dt.float16
I32 = mybir.dt.int32
U32 = mybir.dt.uint32
U8 = mybir.dt.uint8
ACT = mybir.ActivationFunctionType
ALU = mybir.AluOpType

P = 128
B, T, D = 8, 256, 128
H, HD = 16, 8
ITEMS = 2 * B
QT = T // P
HALF = H // 2
FEAT = 512
EPS = 1e-5
LAMBDA = 0.01
ROW_MAX = 96
ROW_POS = 97
K_SCORE, K_DIAG, K_OFF = 96, 97, 101
RING = 8
NEG_BIG = -3.0e38
ONE_ONE = 0x3C003C00
SCALE = (HD ** -0.5, D ** -0.5)

ORDER = [HALF * r + 2 * j + e for r in range(2) for e in range(2) for j in range(4)]


def layer_of(item):
    return item // B


def pairs(items):
    return items + max(0, items - B)


def build(nc, a):
    with ExitStack() as ctx:
        program(nc, ctx, a)


def program(nc, ctx, a):
    def sb(name, shape, dt=F32):
        return ctx.enter_context(nc.sbuf_tensor(name, shape, dt))

    def sem(name):
        return ctx.enter_context(nc.semaphore(name))

    def need(eng, semaphore, value):
        if value > 0:
            eng.wait_ge(semaphore, value)

    x_sb = sb("x_sb", [P, B * QT, D])
    ident = sb("ident", [P, P])
    w0_raw = sb("w0_raw", [P, 4, D])
    ffn0_raw = sb("ffn0_raw", [P, 3, D])
    w1_raw = sb("w1_raw", [P, 4, D])
    down_raw = sb("down_raw", [P, 32])
    up_raw = sb("up_raw", [32, 2, D])
    bool_raw = sb("bool_raw", [P, 6 * FEAT + 4 * D], U8)
    bias0_rows = sb("bias0_rows", [3, D])
    bias0_cols = sb("bias0_cols", [P, 3])
    bo_row = sb("bo_row", [1, D])
    bf_row = sb("bf_row", [1, D])
    s_cols = sb("s_cols", [P, 3])
    s2_cols = sb("s2_cols", [P, 3])
    w0_t = sb("w0_t", [P, 4, D])
    wkv = sb("wkv", [P, D])
    wt2 = sb("wt2", [P, 2, D])
    down_t = sb("down_t", [32, D])
    wa_t = sb("wa_t", [P, D])
    w_eff = sb("w_eff", [P, 3, D])
    bias_row = sb("bias_row", [1, D])
    bias_bc = sb("bias_bc", [P, D])
    bq_s = sb("bq_s", [P, 2])
    ones_row = sb("ones_row", [1, P])
    eps_c = sb("eps_c", [P, QT])
    mhalf = sb("mhalf", [P, QT])
    al = sb("al", [P, H + 1])
    al_tmp = sb("al_tmp", [P, 4, H + 1])
    toe_i = sb("toe_i", [P, 3 * P], I32)
    toe = sb("toe", [P, 3 * P])
    toe_abs = sb("toe_abs", [P, 3 * P])
    toe_min = sb("toe_min", [P, 3 * P])
    cen_i = sb("cen_i", [P, T], I32)
    cen = sb("cen", [P, T])
    adist = sb("adist", [P, H, 3 * P])
    ratio = sb("ratio", [P, 3 * P])
    rowscale = sb("rowscale", [P, 4, T])
    dist16 = sb("dist16", [P, P], F16)
    al_id = sb("al_id", [P, 2, H, P], F16)
    al16 = sb("al16", [P, H], F16)
    alf = sb("alf", [P, 2, H])
    upos = sb("upos", [H, 3, T])
    upos16 = sb("upos16", [H, 2, T], F16)
    masks = sb("masks", [P, 2, P])
    w_ff0 = sb("w_ff0", [P, FEAT], F16)
    w_ff1 = sb("w_ff1", [P, 4, FEAT], F16)
    w_ff2 = sb("w_ff2", [P, 4, D], F16)
    stack = sb("stack", [P, 2, 4, H, T], F16)
    vpad = sb("vpad", [P, 2, QT, H, 32])
    probs = sb("probs", [P, RING, QT, T])
    red_out = sb("red_out", [P, 4, T], F16)
    qk_sb = sb("qk_sb", [P, 2, T])
    xf = sb("xf", [P, 4, T])
    parts = sb("parts", [P, 2, 4, T], F16)
    stats = sb("stats", [P, QT, 6])
    mv = sb("mv", [P, QT, 2])
    vpe = sb("vpe", [P, QT])
    rstd = sb("rstd", [P, QT])
    xn = sb("xn", [P, QT, D])
    xn_t = sb("xn_t", [P, 2, T])
    mx = sb("mx", [P, 2 * H])
    negmax = sb("negmax", [2 * HALF, 2, P], F16)
    acc_sb = sb("acc_sb", [P, 2 * T])
    rden = sb("rden", [P, 4, 8])
    att = sb("att", [P, QT, D])
    att_t = sb("att_t", [P, T])
    fstats = sb("fstats", [P, QT, 6])
    fmv = sb("fmv", [P, QT, 2])
    fvpe = sb("fvpe", [P, QT])
    frstd = sb("frstd", [P, QT])
    fxn = sb("fxn", [P, QT, D])
    fxn_t = sb("fxn_t", [P, T])
    fth = sb("fth", [P, T])
    fx16 = sb("fx16", [P, 2, T], F16)
    spare = adist[:, :, :].rearrange("p h c -> p (h c)")
    fr = spare[:, 0:4 * T].rearrange("p (g c) -> p g c", g=2)
    fh = spare[:, 4 * T:12 * T].bitcast(F16).rearrange("p (l a k c) -> p l a k c", l=2, a=2, k=4)
    outb = sb("outb", [P, 2, T])

    bank = [ctx.enter_context(nc.psum_tensor(f"bank{i}", [P, 512], F32)) for i in range(8)]
    ps_score, ps_main, ps_alt, ps_acc, ps_m0, ps_m1 = bank[0:2], bank[2:4], bank[4], bank[5], bank[6], bank[7]

    def dram(name, shape):
        return nc.dram_tensor(name, shape, F16, kind="Internal").ap()

    dq = [dram(f"dq{p}", [2, H, 2, HD, T]) for p in range(2)]
    dk = [dram(f"dk{p}", [2, 2, H, HD, T]) for p in range(2)]
    dmax = [dram(f"dmax{p}", [2, HALF, T]) for p in range(2)]
    dpos = dram("dpos", [2, H, T])

    x_d = a["L0_attn_x"].rearrange("b (t p) d -> p (b t) d", p=P)
    out_d = a["out"].rearrange("b (t p) d -> p (b t) d", p=P)

    ld_x0 = sem("ld_x0")
    ld_x = sem("ld_x")
    ld_w0 = sem("ld_w0")
    ld_w1 = sem("ld_w1")
    ld_bool = sem("ld_bool")
    ld_bias = sem("ld_bias")
    ld_s = sem("ld_s")
    ld_alpha = sem("ld_alpha")
    al_zero = sem("al_zero")
    id_ready = sem("id_ready")
    iota_ready = sem("iota_ready")
    const_ready = sem("const_ready")
    stack_zero = sem("stack_zero")
    stack_clear = sem("stack_clear")
    vpad_zero = sem("vpad_zero")
    w0_ps = sem("w0_ps")
    w0_sb = sem("w0_sb")
    bq_ready = sem("bq_ready")
    wkv_ready = sem("wkv_ready")
    wp_ps = sem("wp_ps")
    wp_sb = sem("wp_sb")
    brow_ready = sem("brow_ready")
    dve_setup = sem("dve_setup")
    al_abs = sem("al_abs")
    softplus = sem("softplus")
    adist_ready = sem("adist_ready")
    alf_ready = sem("alf_ready")
    al_id_ready = sem("al_id_ready")
    pos_ready = sem("pos_ready")
    pos_stored = sem("pos_stored")
    pos_loaded = sem("pos_loaded")
    toe_min_ready = sem("toe_min_ready")
    tab1_exp = sem("tab1_exp")
    tab1_ready = sem("tab1_ready")
    s2_ready = sem("s2_ready")
    wff_ready = sem("wff_ready")
    ln_stats = sem("ln_stats")
    ln_rstd = sem("ln_rstd")
    ln_xn = sem("ln_xn")
    xnt_ps = sem("xnt_ps")
    xnt_sb = sem("xnt_sb")
    qk_ps = sem("qk_ps")
    qk_out = sem("qk_out")
    xf_scaled = sem("xf_scaled")
    hi_ready = sem("hi_ready")
    lo_ready = sem("lo_ready")
    bounced = sem("bounced")
    ld_l = [[sem("ld_l00"), sem("ld_l01")], [sem("ld_l10"), sem("ld_l11")]]
    ld_u = [[sem("ld_u00"), sem("ld_u01")], [sem("ld_u10"), sem("ld_u11")]]
    v_ps = sem("v_ps")
    v_sb = sem("v_sb")
    score_ps = sem("score_ps")
    red_first = sem("red_first")
    max_ready = sem("max_ready")
    maxt_ps = sem("maxt_ps")
    maxt_sb = sem("maxt_sb")
    max_stored = sem("max_stored")
    max_loaded = sem("max_loaded")
    logits_ps = sem("logits_ps")
    chosen = sem("chosen")
    probs_ready = sem("probs_ready")
    pv_done = sem("pv_done")
    acc_ready = sem("acc_ready")
    acct_ps = sem("acct_ps")
    rden_ready = sem("rden_ready")
    att_ready = sem("att_ready")
    attt_ps = sem("attt_ps")
    attt_sb = sem("attt_sb")
    proj_ps = sem("proj_ps")
    x_biased = sem("x_biased")
    x_attended = sem("x_attended")
    f_stats = sem("f_stats")
    f_rstd = sem("f_rstd")
    f_xn = sem("f_xn")
    ft_ps = sem("ft_ps")
    ft_sb = sem("ft_sb")
    f0_ps = sem("f0_ps")
    f0_tanh = sem("f0_tanh")
    x_ffn0 = sem("x_ffn0")
    f_lo = sem("f_lo")
    h_ps = sem("h_ps")
    h_sb = sem("h_sb")
    h_lo = sem("h_lo")
    h2_ps = sem("h2_ps")
    out_ready = sem("out_ready")
    out_stored = [sem("out_stored0"), sem("out_stored1")]

    def x_item(item):
        b = item % B
        return x_sb[:, b * QT:(b + 1) * QT, :]

    proj = ((w0_t[:, 0, :], w0_t[:, 1, :], w0_t[:, 2, :], w0_t[:, 3, :]),
            (w1_raw[:, 0, :], w_eff[:, 0, :], w_eff[:, 1, :], w1_raw[:, 3, :]))

    def max_loads(groups):
        return 16 * groups + 16 * max(0, groups - 2 * B)

    m_last = [None, None]

    def m_free(pe, m):
        if m_last[m] is not None:
            pe.wait_ge(*m_last[m])

    def pe_scores(pe, it, s):
        h, par = ORDER[s], it % 2
        if s % HALF == 0:
            pe.wait_ge(ld_l[par][s // HALF], 96 * (it // 2 + 1))
        need(pe, max_ready, 16 * it + s - 1)
        for t in range(QT):
            mm = pe.matmul(ps_score[s % 2][:, t * T:(t + 1) * T], stack[0:K_SCORE, par, 0, h, t * P:(t + 1) * P],
                           stack[0:K_SCORE, par, 1, h, :], start=True, stop=True)
        mm.then_inc(score_ps, 1)

    def pe_logits(pe, it, s):
        h, par = ORDER[s], it % 2
        c = 16 * it + s
        if s % HALF == 0:
            pe.wait_ge(max_loaded, max_loads(2 * it + s // HALF + 1))
            if layer_of(it):
                pe.wait_ge(ld_u[par][s // HALF], 96 * ((it - B) // 2 + 1))
        need(pe, probs_ready, c - 1)
        main = ps_main[s % 2]

        def key(v, rows, t):
            return stack[0:rows, par, v, h, t * P:(t + 1) * P]

        def query(v, rows, lo, hi):
            return stack[0:rows, par, v, h, lo:hi]

        if layer_of(it) == 0:
            if c == 0:
                pe.wait_ge(pos_loaded, 64)
                pe.wait_ge(al_id_ready, 1)
            for t in range(QT):
                o = 1 - t
                d0, f0 = t * T + t * P, t * T + o * P
                pe.matmul(main[:, d0:d0 + P], key(1, K_DIAG, t), query(0, K_DIAG, t * P, t * P + P), start=True, stop=False)
                pe.matmul(main[:, d0:d0 + P], dist16[:, :], al_id[:, 0, h, :], start=False, stop=False)
                pe.matmul(main[:, d0:d0 + P], dist16[:, :], al_id[:, 1, h, :], start=False, stop=True)
                mm = pe.matmul(main[:, f0:f0 + P], key(1, K_OFF, t), query(0, K_OFF, o * P, o * P + P), start=True, stop=True)
        else:
            pe.matmul(main[:, 0:T], key(1, K_DIAG, 0), query(0, K_DIAG, 0, T), start=True, stop=True)
            pe.matmul(main[:, T:2 * T], key(3, K_DIAG, 1), query(2, K_DIAG, 0, T), start=True, stop=True)
            need(pe, chosen, c - 16 * B)
            pe.matmul(ps_alt[:, 0:P], key(3, K_DIAG, 0), query(2, K_DIAG, 0, P), start=True, stop=True)
            mm = pe.matmul(ps_alt[:, P:2 * P], key(1, K_DIAG, 1), query(0, K_DIAG, P, T), start=True, stop=True)
        mm.then_inc(logits_ps, 1)

    def pe_pv(pe, it, g):
        need(pe, probs_ready, 16 * it + 4 * g + 4)
        if g == 0:
            need(pe, acc_ready, it)
            pe.wait_ge(v_sb, it + 1)
        r, e = g // 2, g % 2
        for t in range(QT):
            for j in range(4):
                mm = pe.matmul(ps_acc[32 * j:32 * j + 32, r * T:(r + 1) * T],
                               vpad[:, it % 2, t, HALF * r + 2 * j + e, :], probs[:, (4 * g + j) % RING, t, :],
                               start=(e == 0 and t == 0), stop=(e == 1 and t == 1))
        mm.then_inc(pv_done, 1)

    def pe_max_t(pe, it, half):
        pe.wait_ge(max_ready, 16 * it + 8 * half + 8)
        m_free(pe, 0)
        pe.transpose(ps_m0[0:16, 0:P], mx[:, 16 * half:16 * half + 16], ident[:, :]).then_inc(maxt_ps, 1)
        m_last[0] = (maxt_sb, 2 * it + half + 1)

    def pe_transpose_pair(pe, m, src):
        ps = (ps_m0, ps_m1)[m]
        for t in range(QT):
            mm = pe.transpose(ps[:, t * P:(t + 1) * P], src[:, t, :], ident[:, :])
        return mm

    def pe_hidden(pe, it, g):
        m = 1 if g == 3 else 0
        ps = (ps_m0, ps_m1)[m]
        n1 = it - B
        if g == 0:
            pe.wait_ge(f_lo, n1 + 1)
        if g == 2:
            pe.wait_ge(h_lo, 4 * n1 + 2)
        m_free(pe, m)
        for j in range(2):
            k0 = (2 * (g % 2) + j) * P
            terms = [(w_ff0[:, k0:k0 + P], fx16[:, p, :]) for p in range(2)] if g < 2 else \
                    [(w_ff1[:, k, k0:k0 + P], fh[:, 0, p, k, :]) for k in range(4) for p in range(2)]
            for n, (w, v) in enumerate(terms):
                mm = pe.matmul(ps[:, j * T:(j + 1) * T], w, v, start=(n == 0), stop=(n == len(terms) - 1))
        mm.then_inc(h_ps, 1)
        m_last[m] = (h_sb, 4 * n1 + g + 1)

    def pe_iteration(pe, i):
        for s in range(H):
            if s == 0 and has(i + 1):
                pe.wait_ge(xnt_sb, i + 2)
                m_free(pe, 1)
                for w in range(2):
                    mm = pe.matmul(ps_m1[:, w * T:(w + 1) * T], proj[layer_of(i + 1)][w], xn_t[:, (i + 1) % 2, :],
                                   start=True, stop=True)
                mm.then_inc(qk_ps, 1)
                m_last[1] = (qk_out, i + 2)
            if has(i):
                pe_scores(pe, i, s)
            if has(i - 1):
                pe_logits(pe, i - 1, s)
            if s % 4 == 1 and s > 1 and has(i - 1):
                pe_pv(pe, i - 1, s // 4 - 1)
            if s == 1:
                if has(i - 2):
                    pe_pv(pe, i - 2, 3)
                if has(i - 1):
                    pe_max_t(pe, i - 1, 1)
            if s == 2 and has(i):
                m_free(pe, 1)
                for t in range(QT):
                    mm = pe.matmul(ps_m1[:, t * D:(t + 1) * D], xn_t[:, i % 2, t * P:(t + 1) * P], proj[layer_of(i)][2],
                                   start=True, stop=True)
                mm.then_inc(v_ps, 1)
                m_last[1] = (v_sb, i + 1)
            if s == 4 and has(i - 3):
                pe.wait_ge(f_xn, i - 2)
                m_free(pe, 0)
                pe_transpose_pair(pe, 0, fxn).then_inc(ft_ps, 1)
                m_last[0] = (ft_sb, i - 2)
            if s == 4 and has(i - 2):
                pe.wait_ge(acc_ready, i - 1)
                m_free(pe, 1)
                for blk in range(4):
                    mm = pe.transpose(ps_m1[:, blk * P:(blk + 1) * P], acc_sb[:, blk * P:(blk + 1) * P], ident[:, :])
                mm.then_inc(acct_ps, 1)
                m_last[1] = (att_ready, i - 1)
            if s == 6 and has(i - 3) and layer_of(i - 3) == 0:
                pe.wait_ge(ft_sb, i - 2)
                m_free(pe, 0)
                for t in range(QT):
                    pe.matmul(ps_m0[:, t * D:(t + 1) * D], fxn_t[:, t * P:(t + 1) * P], w_eff[:, 2, :], start=True, stop=False)
                    mm = pe.matmul(ps_m0[:, t * D:(t + 1) * D], ones_row[:, :], bf_row[:, :], start=False, stop=True)
                mm.then_inc(f0_ps, 1)
                m_last[0] = (f0_tanh, i - 2)
            if s == 6 and has(i - 2):
                pe.wait_ge(att_ready, i - 1)
                m_free(pe, 1)
                pe_transpose_pair(pe, 1, att).then_inc(attt_ps, 1)
                m_last[1] = (attt_sb, i - 1)
            if s in (7, 8) and has(i - 3) and layer_of(i - 3) == 1:
                pe_hidden(pe, i - 3, s - 7)
            if s == 8 and has(i - 2):
                pe.wait_ge(attt_sb, i - 1)
                m_free(pe, 1)
                for t in range(QT):
                    mm = pe.matmul(ps_m1[:, t * D:(t + 1) * D], att_t[:, t * P:(t + 1) * P], proj[layer_of(i - 2)][3],
                                   start=True, stop=True)
                mm.then_inc(proj_ps, 1)
                m_last[1] = (x_attended, i - 1)
            if s == 9 and has(i):
                pe_max_t(pe, i, 0)
            if s == 10 and has(i - 4) and layer_of(i - 4) == 1:
                pe.wait_ge(h_lo, 4 * (i - 3 - B))
                m_free(pe, 1)
                for t in range(QT):
                    for n, (k, p) in enumerate([(k, p) for k in range(4) for p in range(2)]):
                        mm = pe.matmul(ps_m1[:, t * D:(t + 1) * D], fh[:, 1, p, k, t * P:(t + 1) * P], w_ff2[:, k, :],
                                       start=(n == 0), stop=(n == 7))
                mm.then_inc(h2_ps, 1)
                m_last[1] = (out_ready, i - 3 - B)
            if s in (12, 13) and has(i - 3) and layer_of(i - 3) == 1:
                pe_hidden(pe, i - 3, s - 10)
            if s == 14 and has(i + 2):
                pe.wait_ge(ln_xn, i + 3)
                m_free(pe, 0)
                pe_transpose_pair(pe, 0, xn).then_inc(xnt_ps, 1)
                m_last[0] = (xnt_sb, i + 3)

    def dve_stats(dve, it, x, st, semaphore):
        for t in range(QT):
            dve.bn_stats(st[:, t, :], x[:, t, :]).then_inc(semaphore, 1)

    def dve_mean(dve, it, st, m, semaphore):
        dve.wait_ge(semaphore, 4 * it + 2)
        for t in range(QT):
            dve.bn_aggr(m[:, t, :], st[:, t, :]).then_inc(semaphore, 1)

    def dve_normalize(dve, x, m, r, out):
        for t in range(QT):
            ts = dve.tensor_scalar(out[:, t, :], x[:, t, :], m[:, t, 0:1], r[:, t:t + 1], ALU.subtract, ALU.mult)
        return ts

    def dve_iteration(dve, i):
        for s in range(H):
            if has(i - 1) and layer_of(i - 1) == 1:
                dve.wait_ge(logits_ps, 16 * (i - 1) + s + 1)
                diag = ps_main[s % 2][:, :].rearrange("p (a c) -> p a c", a=4)[:, 0:4:3, :]
                dve.copy_predicated(diag, masks[:, :, :].bitcast(U32),
                                    ps_alt[:, 0:2 * P].rearrange("p (a c) -> p a c", a=2)).then_inc(chosen, 1)
            if has(i):
                h = ORDER[s]
                dve.wait_ge(score_ps, 16 * i + s + 1)
                if s % HALF == 0:
                    need(dve, maxt_ps, 2 * i - 1 + s // HALF)
                one = layer_of(i) == 1
                tab = ratio[:, :] if one else adist[:, h, :]
                for t in range(QT):
                    dve.tensor_tensor_reduce(
                        red_out[:, (2 * s + t) % 4, :], ps_score[s % 2][:, t * T:(t + 1) * T],
                        tab[:, (1 - t) * P:(1 - t) * P + T], 1.0, NEG_BIG, ALU.mult if one else ALU.add, ALU.max,
                        mx[:, 2 * h + t:2 * h + t + 1]).then_inc(max_ready if t == 1 else red_first, 1)
            if has(i - 3):
                f = i - 3
                if s == 0:
                    dve.wait_ge(x_attended, f + 1)
                    dve_stats(dve, f, x_item(f), fstats, f_stats)
                if s == 1:
                    need(dve, f_xn, f)
                    dve_mean(dve, f, fstats, fmv, f_stats)
                if s == 3:
                    dve.wait_ge(f_rstd, 2 * (f + 1))
                    need(dve, ft_ps, f)
                    dve_normalize(dve, x_item(f), fmv, frstd, fxn).then_inc(f_xn, 1)
            if has(i + 1):
                n = i + 1
                if s == 3:
                    if layer_of(n) == 0:
                        dve.wait_ge(qk_out, n + 1)
                    else:
                        dve.wait_ge(xf_scaled, 2 * (n - B) + 1)
                    need(dve, bounced, 48 * pairs(n))
                    dve.tensor_copy(parts[:, 0, 0:2, :], xf[:, 0:2, :]).then_inc(hi_ready, 1)
                if s == 6 and layer_of(n) == 1:
                    dve.wait_ge(xf_scaled, 2 * (n - B) + 2)
                    dve.tensor_copy(parts[:, 0, 2:4, :], xf[:, 2:4, :]).then_inc(hi_ready, 1)
            if has(i - 2):
                m = i - 2
                if s == 5:
                    dve.wait_ge(acct_ps, m + 1)
                    den = ps_m1[:, :].rearrange("p (b j c) -> p b j c", b=4, c=16)
                    dve.reciprocal(rden[:, :, :], den[:, :, :, HD]).then_inc(rden_ready, 1)
                    dve.wait_ge(rden_ready, m + 1)
                    need(dve, attt_ps, m)
                    for t in range(QT):
                        num = ps_m1[:, :].rearrange("p (r t j c) -> p t r j c", r=2, t=2, c=16)[:, t, :, :, 0:HD]
                        rd = rden[:, t:4:2, :].unsqueeze(3).to_broadcast([P, 2, 8, HD])
                        tt = dve.tensor_tensor(att[:, t, :].rearrange("p (r j c) -> p r j c", r=2, c=HD), num, rd,
                                               ALU.mult)
                    tt.then_inc(att_ready, 1)
                if s == 9:
                    dve.wait_ge(proj_ps, m + 1)
                    if layer_of(m) == 0:
                        dve.wait_ge(x_biased, m + 1)
                    dve.tensor_tensor(x_item(m), ps_m1[:, 0:T].rearrange("p (t d) -> p t d", t=QT), x_item(m),
                                      ALU.add).then_inc(x_attended, 1)
            if s == 11 and has(i - 4) and layer_of(i - 4) == 1:
                b = i - 4 - B
                dve.wait_ge(h2_ps, b + 1)
                if b >= 2:
                    dve.wait_ge(out_stored[b % 2], 16 * (b // 2))
                dve.scalar_tensor_tensor(out=outb[:, b % 2, :], in0=ps_m1[:, 0:T], scalar=s_cols[:, 2:3],
                                         in1=x_item(b).rearrange("p t d -> p (t d)"),
                                         op0=ALU.mult, op1=ALU.add).then_inc(out_ready, 1)
            if has(i + 2):
                n = i + 2
                if s == 7:
                    if n == 0:
                        dve.wait_ge(ld_x0, 16)
                    elif n == 1:
                        dve.wait_ge(ld_x, 16 * (B - 1))
                    elif layer_of(n) == 1:
                        dve.wait_ge(x_ffn0, n - B + 1)
                    dve_stats(dve, n, x_item(n), stats, ln_stats)
                if s == 8:
                    need(dve, ln_xn, n)
                    dve_mean(dve, n, stats, mv, ln_stats)
                if s == 12:
                    dve.wait_ge(ln_rstd, 2 * (n + 1))
                    need(dve, xnt_ps, n)
                    dve_normalize(dve, x_item(n), mv, rstd, xn).then_inc(ln_xn, 1)

    def max_store(eng, it, half):
        eng.wait_ge(maxt_sb, 2 * it + half + 1)
        need(eng, max_loaded, max_loads(2 * it + half + 1 - 4))
        eng.dma_start(dmax[it % 2][half].rearrange("h (t q) -> (h t) q", t=QT), negmax[:, half, :]).then_inc(max_stored, 16)

    def max_load(eng, it, half):
        eng.wait_ge(max_stored, 16 * (2 * it + half + 1))
        for v in range(1 + layer_of(it)):
            eng.dma_start(stack[ROW_MAX:ROW_MAX + 1, it % 2, 2 * v, HALF * half:HALF * (half + 1), :],
                          dmax[it % 2][half:half + 1]).then_inc(max_loaded, 16)

    def act_max(act, it, half):
        act.wait_ge(maxt_ps, 2 * it + half + 1)
        need(act, max_stored, 16 * (2 * it + half - 1))
        act.activation(negmax[:, half, :], ps_m0[0:16, 0:P], ACT.Copy, scale=-1.0).then_inc(maxt_sb, 1)

    def act_hidden(act, it, g):
        n = 4 * (it - B) + g
        act.wait_ge(h_ps, n + 1)
        if g == 0:
            act.wait_ge(s2_ready, 1)
        need(act, h_lo, n - 1)
        if g in (0, 1):
            need(act, h_ps, 4 * (it - B))
        else:
            need(act, h2_ps, it - B)
        l = g // 2
        act.activation(fh[:, l, 0, 2 * (g % 2):2 * (g % 2) + 2, :],
                       (ps_m1 if g == 3 else ps_m0)[:, :].rearrange("p (k c) -> p k c", k=2), ACT.Relu,
                       scale=s2_cols[:, l:l + 1])
        act.activation(fr[:, g % 2, :], (ps_m1 if g == 3 else ps_m0)[:, :], ACT.Relu,
                       scale=s2_cols[:, l:l + 1]).then_inc(h_sb, 1)

    def act_iteration(act, i):
        for s in range(H):
            if has(i - 1):
                c = 16 * (i - 1) + s
                if layer_of(i - 1) == 1:
                    act.wait_ge(chosen, c - 16 * B + 1)
                else:
                    act.wait_ge(logits_ps, c + 1)
                if s % 4 == 0:
                    need(act, pv_done, c // 4 - 1)
                act.activation(probs[:, s % RING, :, :], ps_main[s % 2][:, :].rearrange("p (a c) -> p a c", a=2),
                               ACT.Exp).then_inc(probs_ready, 1)
            if s == 1 and has(i + 1):
                n = i + 1
                act.wait_ge(qk_ps, n + 1)
                if layer_of(n) == 0:
                    if n == 0:
                        act.wait_ge(bq_ready, 1)
                    need(act, lo_ready, n)
                    act.activation(xf[:, 0, :], ps_m1[:, 0:T], ACT.Identity, bias=bq_s[:, 0:1], scale=SCALE[0])
                    act.activation(xf[:, 1, :], ps_m1[:, T:2 * T], ACT.Identity, bias=bq_s[:, 1:2]).then_inc(qk_out, 1)
                else:
                    need(act, xf_scaled, 2 * (n - B))
                    act.activation(qk_sb[:, :, :].rearrange("p a c -> p (a c)"), ps_m1[:, :], ACT.Copy).then_inc(qk_out, 1)
            if s == 2 and has(i - 2):
                act.wait_ge(pv_done, 4 * (i - 1))
                need(act, acct_ps, i - 2)
                act.activation(acc_sb[:, :], ps_acc[:, :], ACT.Copy).then_inc(acc_ready, 1)
            if s == 2 and has(i - 1):
                act_max(act, i - 1, 1)
            if s == 3 and has(i):
                act.wait_ge(v_ps, i + 1)
                need(act, pv_done, 4 * (i - 1))
                if i == 0:
                    act.wait_ge(const_ready, 2)
                dst = vpad[:, i % 2, :, :, :].rearrange("p t (g e) (f c) -> p (t g) e f c", e=2, f=2)
                src = ps_m1[:, 0:T].rearrange("p (g e c) -> p g e c", e=2, c=HD)
                for e in range(2):
                    cp = act.activation(dst[:, :, e, e, 0:HD], src[:, :, e, :], ACT.Copy)
                cp.then_inc(v_sb, 1)
            if s == 3 and has(i - 1):
                max_store(act, i - 1, 1)
            if s == 5 and has(i - 3):
                f = i - 3
                act.wait_ge(ft_ps, f + 1)
                if layer_of(f) == 0:
                    need(act, f0_ps, f)
                else:
                    need(act, f_lo, f - B)
                    if f == B:
                        act.wait_ge(f0_ps, B)
                    need(act, h_ps, 4 * (f - B) - 2)
                    act.activation(fx16[:, 0, :], ps_m0[:, 0:T], ACT.Copy)
                act.activation(fxn_t[:, :], ps_m0[:, 0:T], ACT.Copy).then_inc(ft_sb, 1)
            if s == 5 and has(i - 1):
                max_load(act, i - 1, 1)
            if s == 7 and has(i - 2):
                act.wait_ge(attt_ps, i - 1)
                need(act, proj_ps, i - 2)
                act.activation(att_t[:, :], ps_m1[:, 0:T], ACT.Copy).then_inc(attt_sb, 1)
            if s == 7 and has(i - 3) and layer_of(i - 3) == 0:
                act.wait_ge(f0_ps, i - 2)
                need(act, x_ffn0, i - 3)
                act.activation(fth[:, :], ps_m0[:, 0:T], ACT.Tanh).then_inc(f0_tanh, 1)
            if s in (7, 8) and has(i - 3) and layer_of(i - 3) == 1:
                act_hidden(act, i - 3, s - 7)
            if s == 10 and has(i):
                act_max(act, i, 0)
            if s == 11 and has(i):
                max_store(act, i, 0)
            if s == 13 and has(i):
                max_load(act, i, 0)
            if s in (13, 14) and has(i - 3) and layer_of(i - 3) == 1:
                act_hidden(act, i - 3, s - 11)
            if s == 15 and has(i + 2):
                act.wait_ge(xnt_ps, i + 3)
                need(act, v_ps, i + 1)
                act.activation(xn_t[:, i % 2, :], ps_m0[:, 0:T], ACT.Copy).then_inc(xnt_sb, 1)

    def pool_rstd(pool, it, m, v, r, st_sem, r_sem, xn_sem):
        pool.wait_ge(st_sem, 4 * (it + 1))
        need(pool, xn_sem, it)
        pool.tensor_tensor(v[:, :], m[:, :, 1], eps_c[:, :], ALU.add).then_inc(r_sem, 1)
        pool.wait_ge(r_sem, 2 * it + 1)
        pool.tensor_tensor(r[:, :], v[:, :], mhalf[:, :], ALU.pow).then_inc(r_sem, 1)

    def pool_low(pool, k, v):
        pool.wait_ge(hi_ready, k + 1)
        pool.tensor_tensor(parts[:, 1, v:v + 2, :], xf[:, v:v + 2, :], parts[:, 0, v:v + 2, :],
                           ALU.subtract).then_inc(lo_ready, 1)

    def pool_scale(pool, n, form):
        if form == 0:
            pool.wait_ge(qk_out, n + 1)
            if n == B:
                pool.wait_ge(tab1_ready, 1)
                pool.wait_ge(lo_ready, B)
        pool.tensor_tensor(xf[:, 2 * form:2 * form + 2, :], qk_sb[:, :, :], rowscale[:, 2 * form:2 * form + 2, :],
                           ALU.mult).then_inc(xf_scaled, 1)

    def pool_hidden(pool, it, g):
        n = 4 * (it - B) + g
        pool.wait_ge(h_sb, n + 1)
        l, k = g // 2, 2 * (g % 2)
        pool.tensor_tensor(fh[:, l, 1, k:k + 2, :], fr[:, g % 2, :].rearrange("p (k c) -> p k c", k=2),
                           fh[:, l, 0, k:k + 2, :], ALU.subtract).then_inc(h_lo, 1)

    def pool_iteration(pool, i):
        f, n = i - 3, i + 1
        if has(f):
            pool_rstd(pool, f, fmv, fvpe, frstd, f_stats, f_rstd, f_xn)
        if has(n):
            if layer_of(n) == 0:
                pool_low(pool, n, 0)
            else:
                pool_scale(pool, n, 0)
                pool_low(pool, pairs(n), 0)
                pool_scale(pool, n, 1)
        if has(f) and layer_of(f) == 1:
            pool.wait_ge(ft_sb, f + 1)
            pool.tensor_tensor(fx16[:, 1, :], fxn_t[:, :], fx16[:, 0, :], ALU.subtract).then_inc(f_lo, 1)
        if has(n) and layer_of(n) == 1:
            pool_low(pool, pairs(n) + 1, 2)
        if has(f) and layer_of(f) == 0:
            pool.wait_ge(f0_tanh, f + 1)
            pool.tensor_tensor(x_item(f), x_item(f), fth[:, :].rearrange("p (t d) -> p t d", t=QT),
                               ALU.add).then_inc(x_ffn0, 1)
        if has(f) and layer_of(f) == 1:
            pool_hidden(pool, f, 0)
        if has(i + 2):
            pool_rstd(pool, i + 2, mv, vpe, rstd, ln_stats, ln_rstd, ln_xn)
        if has(f) and layer_of(f) == 1:
            pool_hidden(pool, f, 1)
        if 2 <= i + 2 < B:
            pool.wait_ge(ln_xn, i + 3)
            pool.tensor_tensor(x_item(i + 2), x_item(i + 2), bias_bc[:, :].unsqueeze(1).to_broadcast([P, QT, D]),
                               ALU.add).then_inc(x_biased, 1)
        if has(f) and layer_of(f) == 1:
            pool_hidden(pool, f, 2)
            pool_hidden(pool, f, 3)

    def sp_bounce(sp, n, form):
        k = pairs(n) + form
        sp.wait_ge(lo_ready, k + 1)
        par = n % 2
        for half in range(2):
            need(sp, (ld_u if form else ld_l)[par][half], 96 * ((n - B if form else n) // 2))
        for p in range(2):
            sp.dma_start(dq[par][form, :, p, :, :], parts[:, p, 2 * form, :]).then_inc(bounced, 16)
        sp.dma_start(dk[par][form].rearrange("p h d t -> (h d) p t"), parts[:, :, 2 * form + 1, :]).then_inc(bounced, 16)
        sp.wait_ge(bounced, 48 * (k + 1))

    def sp_stack(sp, n, form, half):
        par = n % 2
        hs = slice(HALF * half, HALF * (half + 1))
        done = (ld_u if form else ld_l)[par][half]
        need(sp, logits_ps, 16 * (n - 2) + 8 * (half + 1))
        if form == 1 and n == B:
            sp.wait_ge(stack_clear, 4)
        for rep in range(2):
            sp.dma_start(stack[16 * rep:16 * rep + 16, par, 2 * form, hs, :],
                         dq[par][form, hs].rearrange("h p d t -> (p d) h t")).then_inc(done, 16)
            for p in range(2):
                r0 = 16 * p + 8 * rep
                sp.dma_start(stack[r0:r0 + 8, par, 2 * form + 1, hs, :],
                             dk[par][form, p, hs].rearrange("h d t -> d h t")).then_inc(done, 16)

    def sp_iteration(sp, i):
        n = i + 1
        if has(n):
            sp_bounce(sp, n, 0)
            if n < 2:
                sp.wait_ge(stack_clear, n + 1)
            sp_stack(sp, n, 0, 0)
            if layer_of(n) == 1:
                sp_bounce(sp, n, 1)
                sp_stack(sp, n, 1, 0)
        if has(i - 4) and layer_of(i - 4) == 1:
            b = i - 4 - B
            sp.wait_ge(out_ready, b + 1)
            sp.dma_start(out_d[:, b * QT:(b + 1) * QT, :],
                         outb[:, b % 2, :].rearrange("p (t d) -> p t d", t=QT)).then_inc(out_stored[b % 2], 16)
        if has(n):
            sp_stack(sp, n, 0, 1)
            if layer_of(n) == 1:
                sp_stack(sp, n, 1, 1)

    def has(item):
        return 0 <= item < ITEMS

    LAST = ITEMS + 4

    block = ctx.enter_context(nc.Block())

    @block.sync
    def _(sp):
        sp.dma_start(x_sb[:, 0:QT, :], x_d[:, 0:QT, :]).then_inc(ld_x0, 16)
        sp.dma_start(w0_raw[:, 0:3, :], a["L0_attn_qkv_w"].rearrange("(n p) d -> p n d", p=P)).then_inc(ld_w0, 16)
        sp.dma_start(w0_raw[:, 3, :], a["L0_attn_out_w"]).then_inc(ld_w0, 16)
        sp.dma_start(bias0_rows[:, :], a["L0_attn_qkv_b"].rearrange("(n p) -> n p", p=P)).then_inc(ld_w0, 16)
        sp.wait_ge(al_zero, 1)
        sp.dma_start(al[:, 0:H], a["L0_attn_decay_alpha"].partition_broadcast(P)).then_inc(ld_alpha, 16)
        sp.dma_start(al[0:H, H:H + 1], a["L0_attn_decay_alpha"].rearrange("(h o) -> h o", o=1)).then_inc(ld_alpha, 16)
        for b in range(1, B):
            sp.dma_start(x_sb[:, QT * b:QT * (b + 1), :], x_d[:, QT * b:QT * (b + 1), :]).then_inc(ld_x, 16)
        sp_iteration(sp, -2)
        sp_iteration(sp, -1)
        for i in range(LAST):
            sp_iteration(sp, i)
        for p in range(2):
            sp.wait_ge(out_stored[p], 16 * B // 2)

    @block.gpsimd
    def _(pool):
        pool.memset(al[:, :], 0.0).then_inc(al_zero, 1)
        pool.memset(ident[:, :], 0.0).then_inc(id_ready, 1)
        pool.wait_ge(id_ready, 1)
        pool.affine_select(out=ident[:, :], in_=ident[:, :], compare_op=ALU.not_equal, fill=1.0, base=0,
                           pattern=[[-1, P]], channel_multiplier=1).then_inc(id_ready, 1)
        pool.iota(toe_i[:, :], [[-1, 3 * P]], base=P, channel_multiplier=1).then_inc(iota_ready, 1)
        pool.iota(cen_i[:, :], [[1, T]], base=-P, channel_multiplier=0).then_inc(iota_ready, 1)
        pool.memset(eps_c[:, :], EPS)
        pool.memset(mhalf[:, :], -0.5)
        pool.memset(ones_row[:, :], 1.0).then_inc(const_ready, 1)
        pool.wait_ge(const_ready, 1)
        pool_rstd(pool, 0, mv, vpe, rstd, ln_stats, ln_rstd, ln_xn)

        def clear(par, v, count):
            pool.memset(stack[0:ROW_MAX, par, v:v + 2, :, :].rearrange("p a h t -> p (a h t)").bitcast(U32),
                        0).then_inc(stack_zero, 1)
            pool.wait_ge(stack_zero, count)
            pool.memset(stack[ROW_MAX:P, par, v:v + 2, :, :].rearrange("p a h t -> p (a h t)").bitcast(U32),
                        ONE_ONE).then_inc(stack_clear, 1)
            pool.wait_ge(stack_clear, count)

        clear(0, 0, 1)
        pool.dma_start(bo_row[:, :], a["L0_attn_out_b"].rearrange("(o n) -> o n", o=1)).then_inc(ld_bias, 16)
        pool.dma_start(bf_row[:, :], a["L0_ffn_bias"].rearrange("(o n) -> o n", o=1)).then_inc(ld_bias, 16)
        pool.memset(vpad[:, :, :, :, :], 0.0).then_inc(vpad_zero, 1)
        pool.wait_ge(vpad_zero, 1)
        for e in range(2):
            ms = pool.memset(vpad[:, :, :, :, :].rearrange("p a t (g e) c -> p (a t g) e c", e=2)
                             [:, :, e, 16 * e + HD:16 * e + HD + 1], 1.0)
        ms.then_inc(const_ready, 1)
        pool_iteration(pool, -1)
        clear(1, 0, 2)
        pool.wait_ge(pos_ready, 1)
        pool.dma_start(dpos.rearrange("n h t -> h n t"), upos16[:, :, :]).then_inc(pos_stored, 16)
        pool.wait_ge(pos_stored, 16)
        for par in range(2):
            pool.dma_start(stack[ROW_POS:ROW_POS + 2, par, 0, :, :], dpos).then_inc(pos_loaded, 16)
            pool.dma_start(stack[ROW_POS + 2:ROW_POS + 4, par, 1, :, :], dpos).then_inc(pos_loaded, 16)
        pool.wait_ge(wp_sb, 2)
        for it in range(2):
            pool.wait_ge(ln_xn, it + 1)
            pool.tensor_tensor(x_item(it), x_item(it), bias_bc[:, :].unsqueeze(1).to_broadcast([P, QT, D]),
                               ALU.add).then_inc(x_biased, 1)
        for i in range(LAST):
            pool_iteration(pool, i)
            if i in (0, 1):
                clear(i, 2, 3 + i)

    @block.vector
    def _(dve):
        done = [0]

        def step(ins):
            done[0] += 1
            ins.then_inc(dve_setup, 1)
            dve.wait_ge(dve_setup, done[0])

        dve_iteration(dve, -2)
        dve.wait_ge(ld_alpha, 32)
        step(dve.tensor_scalar(al_tmp[:, 0, :], al[:, :], -1.0, None, ALU.mult))
        dve.tensor_tensor(al_tmp[:, 1, :], al[:, :], al_tmp[:, 0, :], ALU.max).then_inc(al_abs, 1)
        dve.wait_ge(w0_sb, 1)
        dve.tensor_scalar(bq_s[:, 0:1], bias0_cols[:, 0:1], SCALE[0], None, ALU.mult)
        dve.tensor_copy(bq_s[:, 1:2], bias0_cols[:, 1:2]).then_inc(bq_ready, 1)
        dve.wait_ge(iota_ready, 2)
        dve.tensor_copy(toe[:, :], toe_i[:, :])
        step(dve.tensor_copy(cen[:, :], cen_i[:, :]))
        dve.tensor_scalar(toe_abs[:, :], toe[:, :], -1.0, None, ALU.mult)
        step(dve.tensor_scalar(upos[:, 0, :], cen[0:H, :], -1.0, None, ALU.mult))
        dve.tensor_tensor(toe_abs[:, :], toe[:, :], toe_abs[:, :], ALU.max)
        step(dve.tensor_tensor(upos[:, 1, :], cen[0:H, :], upos[:, 0, :], ALU.max))
        dve_iteration(dve, -1)
        dve.wait_ge(softplus, 2)
        step(dve.scalar_tensor_tensor(out=al_tmp[:, 0, :], in0=al[:, :], scalar=0.0, in1=al_tmp[:, 3, :],
                                      op0=ALU.max, op1=ALU.add))
        step(dve.tensor_scalar(al_tmp[:, 1, :], al_tmp[:, 0, :], -1.0, None, ALU.mult))
        for h in ORDER:
            ts = dve.tensor_scalar(adist[:, h, :], toe_abs[:, :], al_tmp[:, 1, h:h + 1], None, ALU.mult)
        ts.then_inc(adist_ready, 1)
        step(dve.tensor_scalar(upos[:, 2, :], upos[:, 1, :], al_tmp[0:H, 1, H:H + 1], None, ALU.mult))
        step(dve.tensor_copy(upos16[:, 0, :], upos[:, 2, :]))
        dve.tensor_tensor(upos16[:, 1, :], upos[:, 2, :], upos16[:, 0, :], ALU.subtract).then_inc(pos_ready, 1)
        dve.tensor_scalar(dist16[:, :], toe_abs[:, P:2 * P], -1.0, None, ALU.mult)
        step(dve.tensor_copy(al16[:, :], al_tmp[:, 0, 0:H]))
        step(dve.tensor_copy(alf[:, 0, :], al16[:, :]))
        dve.tensor_tensor(alf[:, 1, :], al_tmp[:, 0, 0:H], alf[:, 0, :], ALU.subtract).then_inc(alf_ready, 1)
        dve.tensor_scalar(toe_min[:, :], toe[:, :], 0.0, None, ALU.min).then_inc(toe_min_ready, 1)
        dve.wait_ge(ld_w1, 160)
        dve.tensor_tensor(wkv[:, :], w1_raw[:, 1, :], w1_raw[:, 2, :], ALU.add).then_inc(wkv_ready, 1)
        dve.wait_ge(ld_bias, 32)
        dve.wait_ge(wp_sb, 1)
        dve.tensor_tensor(bias_row[:, :], ps_alt[0:1, 2 * D:3 * D], bo_row[:, :], ALU.add).then_inc(brow_ready, 1)
        dve.wait_ge(adist_ready, 1)
        dve_iteration(dve, 0)
        dve.tensor_scalar(masks[:, 0, :], toe[:, P:2 * P], 0.0, None, ALU.is_gt)
        dve.tensor_scalar(masks[:, 1, :], toe[:, P:2 * P], 0.0, None, ALU.is_lt)
        dve.wait_ge(tab1_exp, 1)
        for v in (0, 2):
            ts = dve.tensor_scalar(rowscale[:, v, :], rowscale[:, v, :], SCALE[1], None, ALU.mult)
        ts.then_inc(tab1_ready, 1)
        dve.wait_ge(ld_s, 48)
        dve.tensor_scalar(s2_cols[:, :], s_cols[:, :], 2.0, None, ALU.mult).then_inc(s2_ready, 1)
        dve.wait_ge(ld_bool, 48)
        dve.tensor_tensor(w_ff0[:, :], bool_raw[:, 0:FEAT], bool_raw[:, FEAT:2 * FEAT], ALU.subtract).then_inc(wff_ready, 1)
        dve_iteration(dve, 1)
        dve.wait_ge(wff_ready, 1)
        dve.tensor_scalar(w_ff0[:, :], w_ff0[:, :], 2.0, None, ALU.mult).then_inc(wff_ready, 1)
        dve.tensor_scalar(w_ff2[:, :, :].rearrange("p n f -> p (n f)"), bool_raw[:, 6 * FEAT:6 * FEAT + 4 * D], 2.0, -1.0,
                          ALU.mult, ALU.add).then_inc(wff_ready, 1)
        for i in range(2, LAST):
            dve_iteration(dve, i)
            if i in (2, 3, 4, 5):
                k = i - 2
                dve.tensor_scalar(w_ff1[:, k, :], bool_raw[:, (2 + k) * FEAT:(3 + k) * FEAT], 2.0, -1.0,
                                  ALU.mult, ALU.add).then_inc(wff_ready, 1)

    @block.scalar
    def _(act):
        act.wait_ge(w0_ps, 1)
        act.activation(bias0_cols[:, :], ps_m1[:, 0:3], ACT.Copy)
        act.activation(w0_t[:, :, :].rearrange("p n d -> p (n d)"), ps_m0[:, :], ACT.Copy).then_inc(w0_sb, 1)
        act_iteration(act, -2)
        act.wait_ge(al_abs, 1)
        act.activation(al_tmp[:, 2, :], al_tmp[:, 1, :], ACT.Exp, scale=-1.0).then_inc(softplus, 1)
        act.wait_ge(softplus, 1)
        act.activation(al_tmp[:, 3, :], al_tmp[:, 2, :], ACT.Ln, bias=1.0).then_inc(softplus, 1)
        for n, name in enumerate(("L1_attn_W_q", "L1_attn_W_k", "L1_attn_W_v", "L1_attn_W_o")):
            act.dma_start(w1_raw[:, n, :], a[name]).then_inc(ld_w1, 16)
        for n, name in enumerate(("L0_ffn_weight", "L0_ffn_aux_weight1", "L0_ffn_aux_weight2")):
            act.dma_start(ffn0_raw[:, n, :], a[name]).then_inc(ld_w1, 16)
        act.dma_start(down_raw[:, :], a["L1_attn_W_down_kv"]).then_inc(ld_w1, 16)
        act.dma_start(up_raw[:, 0, :], a["L1_attn_W_up_k"]).then_inc(ld_w1, 16)
        act.dma_start(up_raw[:, 1, :], a["L1_attn_W_up_v"]).then_inc(ld_w1, 16)
        act_iteration(act, -1)
        act.wait_ge(wp_ps, 1)
        act.activation(wt2[:, :, :].rearrange("p n d -> p (n d)"), ps_alt[:, 0:2 * D], ACT.Copy).then_inc(wp_sb, 1)
        act.wait_ge(wp_ps, 2)
        act.activation(down_t[:, :], ps_acc[0:32, 0:D], ACT.Copy)
        act.activation(wa_t[:, :], ps_acc[:, D:2 * D], ACT.Copy)
        act.activation(bias_bc[:, :], ps_acc[:, 2 * D:3 * D], ACT.Copy).then_inc(wp_sb, 1)
        act.wait_ge(wp_ps, 3)
        act.activation(w_eff[:, :, :].rearrange("p n d -> p (n d)"), ps_alt[:, 0:3 * D], ACT.Copy).then_inc(wp_sb, 1)
        act.wait_ge(alf_ready, 1)
        act.wait_ge(id_ready, 2)
        for p in range(2):
            for h in ORDER:
                cp = act.activation(al_id[:, p, h, :], ident[:, :], ACT.Copy, scale=alf[:, p, h:h + 1])
        cp.then_inc(al_id_ready, 1)
        act.wait_ge(toe_min_ready, 1)
        act.activation(ratio[:, :], toe_min[:, :], ACT.Exp, scale=2 * LAMBDA)
        for v, sign in enumerate((-1, 1, 1, -1)):
            ex = act.activation(rowscale[:, v, :], cen[:, :], ACT.Exp, scale=sign * LAMBDA)
        ex.then_inc(tab1_exp, 1)
        for n in range(3):
            act.dma_start(s_cols[:, n:n + 1], a[f"L1_ffn_s{n}"].partition_broadcast(P)).then_inc(ld_s, 16)
        act.dma_start(bool_raw[:, 0:2 * FEAT].rearrange("p (n f) -> p n f", n=2),
                      a["L1_ffn_k0"].rearrange("(n p) f -> p n f", p=P)).then_inc(ld_bool, 16)
        act.dma_start(bool_raw[:, 2 * FEAT:6 * FEAT].rearrange("p (n f) -> p n f", n=4),
                      a["L1_ffn_k1"].rearrange("(n p) f -> p n f", p=P)).then_inc(ld_bool, 16)
        act.dma_start(bool_raw[:, 6 * FEAT:6 * FEAT + 4 * D].rearrange("p (n f) -> p n f", n=4),
                      a["L1_ffn_k2"].rearrange("(n p) f -> p n f", p=P)).then_inc(ld_bool, 16)
        for i in range(LAST):
            act_iteration(act, i)

    @block.tensor
    def _(pe):
        pe.wait_ge(ld_w0, 48)
        pe.wait_ge(id_ready, 2)
        for n in range(4):
            pe.transpose(ps_m0[:, n * D:(n + 1) * D], w0_raw[:, n, :], ident[:, :])
        pe.transpose(ps_m1[:, 0:3], bias0_rows[:, :], ident[0:3, 0:3]).then_inc(w0_ps, 1)
        m_last[0] = m_last[1] = (w0_sb, 1)
        pe_iteration(pe, -2)
        pe_iteration(pe, -1)
        pe.wait_ge(wkv_ready, 1)
        pe.transpose(ps_alt[:, 0:D], wkv[:, :], ident[:, :])
        pe.transpose(ps_alt[:, D:2 * D], ffn0_raw[:, 0, :], ident[:, :])
        pe.matmul(ps_alt[0:1, 2 * D:3 * D], bias0_cols[:, 2:3], w0_t[:, 3, :], start=True, stop=True).then_inc(wp_ps, 1)
        pe.wait_ge(wp_sb, 1)
        pe.matmul(ps_acc[0:32, 0:D], down_raw[:, :], wt2[:, 0, :], start=True, stop=True)
        pe.matmul(ps_acc[:, D:2 * D], ffn0_raw[:, 1, :], wt2[:, 1, :], start=True, stop=True)
        pe.wait_ge(brow_ready, 1)
        pe.wait_ge(const_ready, 1)
        pe.matmul(ps_acc[:, 2 * D:3 * D], ones_row[:, :], bias_row[:, :], start=True, stop=True).then_inc(wp_ps, 1)
        pe.wait_ge(wp_sb, 2)
        pe.matmul(ps_alt[:, 0:D], down_t[:, :], up_raw[:, 0, :], start=True, stop=True)
        pe.matmul(ps_alt[:, D:2 * D], down_t[:, :], up_raw[:, 1, :], start=True, stop=True)
        pe.matmul(ps_alt[:, 2 * D:3 * D], wa_t[:, :], ffn0_raw[:, 2, :], start=True, stop=True).then_inc(wp_ps, 1)
        for i in range(LAST):
            pe_iteration(pe, i)
            if i == 0:
                pe.wait_ge(wp_sb, 3)
                pe.wait_ge(ld_bias, 32)
            if i == B + 2:
                pe.wait_ge(wff_ready, 7)


_INS = ['L0_attn_x', 'L0_attn_qkv_w', 'L0_attn_qkv_b', 'L0_attn_out_w', 'L0_attn_out_b', 'L0_attn_decay_alpha',
        'L0_ffn_weight', 'L0_ffn_aux_weight1', 'L0_ffn_aux_weight2', 'L0_ffn_bias', 'L1_attn_W_q', 'L1_attn_W_k',
        'L1_attn_W_v', 'L1_attn_W_o', 'L1_attn_W_down_kv', 'L1_attn_W_up_k', 'L1_attn_W_up_v', 'L1_ffn_k0',
        'L1_ffn_k1', 'L1_ffn_k2', 'L1_ffn_s0', 'L1_ffn_s1', 'L1_ffn_s2']


def kernel(**inputs):
    import numpy as _np
    import concourse.bacc as _bacc
    from concourse import mybir as _mybir
    from concourse.bass_utils import run_bass_kernel_spmd as _run

    nc = _bacc.Bacc("TRN2", target_bir_lowering=False, num_devices=1)
    arrays, aps = {}, {}
    for name in _INS:
        v = _np.ascontiguousarray(inputs[name])
        if v.ndim == 0 or name.startswith("L1_ffn_s"):
            v = v.reshape(1)
        arrays[f"in_{name}_dram"] = v
        aps[name] = nc.dram_tensor(f"in_{name}_dram", v.shape, _mybir.dt.from_np(v.dtype), kind="ExternalInput").ap()
    aps["out"] = nc.dram_tensor("out_0_dram", (8, 256, 128), _mybir.dt.float32, kind="ExternalOutput").ap()
    build(nc, aps)
    r = _run(nc, [arrays], core_ids=[0])
    return r.results[0]["out_0_dram"]
```

```python
from contextlib import ExitStack

import concourse.bass as bass
from concourse import mybir

F32 = mybir.dt.float32
F16 = mybir.dt.float16
I32 = mybir.dt.int32
U32 = mybir.dt.uint32
U8 = mybir.dt.uint8
ACT = mybir.ActivationFunctionType
ALU = mybir.AluOpType

P = 128
B, T, D = 8, 256, 128
H, HD = 16, 8
ITEMS = 2 * B
QT = T // P
HALF = H // 2
FEAT = 512
EPS = 1e-5
LAMBDA = 0.01
SHARED = {"qk": 7, "acc": 7, "att": 7, "max": 7, "proj": 7, "xn": 7, "v": 6, "ft": 6, "f0": 6, "out": 6,
          "h0": 6, "h1": 6, "h2": 6, "h3": 7}
ENDING = {15: {"acc": 4, "att": 0, "proj": 1, "ft": 4, "h0": 6, "h1": 7, "h2": 4, "h3": 6, "out": 7},
          14: {"ft": 2, "h0": 3, "h1": 0, "h2": 1, "h3": 2, "out": 3}}
PART_ROWS = 2 * HD
ROW_MAX = 96
ROW_POS = 97
K_SCORE, K_DIAG, K_OFF = 96, 97, 101
RING = 8
NEG_BIG = -3.0e38

SLOTS = {
    "qk": (1, 1), "qk_out": (1, 1), "v": (3, 3), "v_out": (3, 3), "xn": (14, 13), "xn_out": (14, 14),
    "stats0": (2, 2), "stats1": (2, 2), "mean": (3, 3), "norm": (10, 11), "hi0": (4, 5), "hi1": (6, 6),
    "max": (9, 9), "max_out": (9, 9), "max_load0": (12, 12), "max_load1": (2, 4), "acc_out": (4, 4), "acc": (8, 7),
    "acc_out0": (8, 7), "acc_out1": (9, 7), "acc_out2": (9, 8), "att": (10, 10), "att_out": (10, 10),
    "proj": (13, 12), "proj_out": (13, 12), "f_stats0": (14, 14), "f_stats1": (14, 14), "f_mean": (15, 15),
    "f_norm": (1, 2), "ft": (5, 5), "ft_out": (5, 6), "f0": (7, 7), "f0_out": (7, 9), "h0": (8, 8),
    "h0_out": (8, 8), "h1": (12, 12), "h1_out": (12, 12), "h2_out": (1, 1), "h3_out": (5, 5), "out": (10, 10),
    "out_out": (10, 10),
}
ONE_ONE = 0x3C003C00
SCALE = (HD ** -0.5, D ** -0.5)

ORDER = [HALF * r + 2 * j + e for r in range(2) for e in range(2) for j in range(4)]


def layer_of(item):
    return item // B


ADDED = (1, 3, 5, 7, 11, 13, 15)


def added(s):
    return s % H in ADDED


def added_before(s):
    return sum(added(k) for k in range(s))


def bank_of(step, item):
    if step in ("max", "xn") and item < B:
        return 6
    return ENDING.get(item, SHARED).get(step, SHARED[step])


def pairs(items):
    return items + max(0, items - B)


def build(nc, a):
    with ExitStack() as ctx:
        program(nc, ctx, a)


def program(nc, ctx, a):
    def sb(name, shape, dt=F32):
        return ctx.enter_context(nc.sbuf_tensor(name, shape, dt))

    def sem(name):
        return ctx.enter_context(nc.semaphore(name))

    def need(eng, semaphore, value):
        if value > 0:
            eng.wait_ge(semaphore, value)

    x_sb = sb("x_sb", [P, B * QT, D])
    ident = sb("ident", [P, P])
    w0_raw = sb("w0_raw", [P, 4, D])
    ffn0_raw = sb("ffn0_raw", [P, 3, D])
    w1_raw = sb("w1_raw", [P, 4, D])
    down_raw = sb("down_raw", [P, 32])
    up_raw = sb("up_raw", [32, 2, D])
    bool_raw = sb("bool_raw", [P, 6 * FEAT + 4 * D], U8)
    bias0_rows = sb("bias0_rows", [3, D])
    bias0_cols = sb("bias0_cols", [P, 3])
    bo_row = sb("bo_row", [1, D])
    bf_row = sb("bf_row", [1, D])
    s_cols = sb("s_cols", [P, 3])
    s2_cols = sb("s2_cols", [P, 3])
    w0_t = sb("w0_t", [P, 4, D])
    wkv = sb("wkv", [P, D])
    wt2 = sb("wt2", [P, 2, D])
    down_t = sb("down_t", [32, D])
    wa_t = sb("wa_t", [P, D])
    w_eff = sb("w_eff", [P, 3, D])
    bias_row = sb("bias_row", [1, D])
    bias_bc = sb("bias_bc", [P, D])
    bq_s = sb("bq_s", [P, 2])
    ones_row = sb("ones_row", [1, P])
    eps_c = sb("eps_c", [P, QT])
    mhalf = sb("mhalf", [P, QT])
    minus1 = sb("minus1", [P, QT])
    al = sb("al", [P, H + 1])
    al_tmp = sb("al_tmp", [P, 4, H + 1])
    toe_i = sb("toe_i", [P, 3 * P], I32)
    toe = sb("toe", [P, 3 * P])
    toe_abs = sb("toe_abs", [P, 3 * P])
    toe_min = sb("toe_min", [P, 3 * P])
    cen_i = sb("cen_i", [P, T], I32)
    cen = sb("cen", [P, T])
    adist = sb("adist", [P, H, 3 * P])
    ratio = sb("ratio", [P, 3 * P])
    rowscale = sb("rowscale", [P, 4, T])
    dist16 = sb("dist16", [P, P], F16)
    al_id = sb("al_id", [P, 2, H, P], F16)
    al16 = sb("al16", [P, H], F16)
    alf = sb("alf", [P, 2, H])
    upos = sb("upos", [H, 3, T])
    upos16 = sb("upos16", [H, 2, T], F16)
    masks = sb("masks", [P, 2, P])
    w_ff0 = sb("w_ff0", [P, FEAT], F16)
    w_ff1 = sb("w_ff1", [P, 4, FEAT], F16)
    w_ff2 = sb("w_ff2", [P, 4, D], F16)
    stack = sb("stack", [P, 2, 4, H, T], F16)
    vpad = sb("vpad", [P, 2, QT, H, 32])
    probs = sb("probs", [P, RING, QT, T])
    red_out = sb("red_out", [P, 4, T], F16)
    qk_sb = sb("qk_sb", [P, 2, T])
    xf = sb("xf", [P, 4, T])
    parts = sb("parts", [P, 2, 4, T], F16)
    stats = sb("stats", [P, QT, 6])
    mv = sb("mv", [P, QT, 2])
    vpe = sb("vpe", [P, 2 * QT])
    negmean = sb("negmean", [P, QT])
    rstd = sb("rstd", [P, QT])
    xn = sb("xn", [P, QT, D])
    xn_t = sb("xn_t", [P, 2, T])
    mx = sb("mx", [P, 2 * H])
    negmax = sb("negmax", [2 * HALF, 2, P], F16)
    acc_sb = sb("acc_sb", [P, 2 * T])
    rden = sb("rden", [P, 4, 8])
    att = sb("att", [P, QT, D])
    att_t = sb("att_t", [P, T])
    fstats = sb("fstats", [P, QT, 6])
    fmv = sb("fmv", [P, QT, 2])
    fvpe = sb("fvpe", [P, 2 * QT])
    fnegmean = sb("fnegmean", [P, QT])
    frstd = sb("frstd", [P, QT])
    fxn = sb("fxn", [P, QT, D])
    fxn_t = sb("fxn_t", [P, T])
    fth = sb("fth", [P, T])
    fx16 = sb("fx16", [P, 2, T], F16)
    spare = adist[:, :, :].rearrange("p h c -> p (h c)")
    fr = spare[:, 0:4 * T].rearrange("p (g c) -> p g c", g=2)
    fh = spare[:, 4 * T:12 * T].bitcast(F16).rearrange("p (l a k c) -> p l a k c", l=2, a=2, k=4)
    outb = sb("outb", [P, 2, T])

    bank = [ctx.enter_context(nc.psum_tensor(f"bank{i}", [P, 512], F32)) for i in range(8)]
    ps_score, ps_main, ps_alt, ps_acc = bank[0:2], bank[2:4], bank[4], bank[5]

    def dram(name, shape):
        return nc.dram_tensor(name, shape, F16, kind="Internal").ap()

    dqk = [dram(f"dqk{p}", [4, 2, HD, H, T]) for p in range(2)]
    dmax = [dram(f"dmax{p}", [2, HALF, T]) for p in range(2)]
    dpos = dram("dpos", [2, H, T])

    x_d = a["L0_attn_x"].rearrange("b (t p) d -> p (b t) d", p=P)
    out_d = a["out"].rearrange("b (t p) d -> p (b t) d", p=P)

    ld_x0 = sem("ld_x0")
    ld_x = sem("ld_x")
    ld_w0 = sem("ld_w0")
    ld_w1 = sem("ld_w1")
    ld_bool = sem("ld_bool")
    ld_bias = sem("ld_bias")
    ld_s = sem("ld_s")
    ld_alpha = sem("ld_alpha")
    al_zero = sem("al_zero")
    id_ready = sem("id_ready")
    iota_ready = sem("iota_ready")
    const_ready = sem("const_ready")
    stack_zero = sem("stack_zero")
    stack_ones = sem("stack_ones")
    stack_clear = sem("stack_clear")
    vpad_zero = sem("vpad_zero")
    w0_ps = sem("w0_ps")
    w0_sb = sem("w0_sb")
    bq_ready = sem("bq_ready")
    wkv_ready = sem("wkv_ready")
    wp_ps = sem("wp_ps")
    wp_sb = sem("wp_sb")
    brow_ready = sem("brow_ready")
    dve_setup = sem("dve_setup")
    al_abs = sem("al_abs")
    softplus = sem("softplus")
    adist_ready = sem("adist_ready")
    alf_ready = sem("alf_ready")
    al_id_ready = sem("al_id_ready")
    pos_ready = sem("pos_ready")
    pos_stored = sem("pos_stored")
    pos_loaded = sem("pos_loaded")
    toe_min_ready = sem("toe_min_ready")
    tab1_exp = sem("tab1_exp")
    tab1_ready = sem("tab1_ready")
    s2_ready = sem("s2_ready")
    wff_ready = sem("wff_ready")
    ln_stats = sem("ln_stats")
    ln_rstd = sem("ln_rstd")
    ln_xn = sem("ln_xn")
    xnt_ps = sem("xnt_ps")
    xnt_sb = sem("xnt_sb")
    qk_ps = sem("qk_ps")
    qk_out = sem("qk_out")
    xf_scaled = sem("xf_scaled")
    hi_ready = sem("hi_ready")
    lo_ready = sem("lo_ready")
    bounced = sem("bounced")
    ld_l = [[sem("ld_l00"), sem("ld_l01")], [sem("ld_l10"), sem("ld_l11")]]
    ld_u = [[sem("ld_u00"), sem("ld_u01")], [sem("ld_u10"), sem("ld_u11")]]
    v_ps = sem("v_ps")
    v_sb = sem("v_sb")
    score_ps = sem("score_ps")
    red_first = sem("red_first")
    max_ready = sem("max_ready")
    maxt_ps = sem("maxt_ps")
    maxt_sb = sem("maxt_sb")
    max_stored = sem("max_stored")
    max_loaded = sem("max_loaded")
    logits_ps = sem("logits_ps")
    dist_added = sem("dist_added")
    chosen = sem("chosen")
    probs_ready = sem("probs_ready")
    pv_done = sem("pv_done")
    acc_ready = sem("acc_ready")
    acct_ps = sem("acct_ps")
    rden_ready = sem("rden_ready")
    att_ready = sem("att_ready")
    attt_ps = sem("attt_ps")
    attt_sb = sem("attt_sb")
    proj_ps = sem("proj_ps")
    x_biased = sem("x_biased")
    x_attended = sem("x_attended")
    f_stats = sem("f_stats")
    f_rstd = sem("f_rstd")
    f_xn = sem("f_xn")
    ft_ps = sem("ft_ps")
    ft_sb = sem("ft_sb")
    f0_ps = sem("f0_ps")
    f0_tanh = sem("f0_tanh")
    x_ffn0 = sem("x_ffn0")
    f_lo = sem("f_lo")
    h_ps = sem("h_ps")
    h_sb = sem("h_sb")
    h_lo = sem("h_lo")
    h2_ps = sem("h2_ps")
    out_ready = sem("out_ready")
    out_stored = [sem("out_stored0"), sem("out_stored1")]

    def x_item(item):
        b = item % B
        return x_sb[:, b * QT:(b + 1) * QT, :]

    proj = ((w0_t[:, 0, :], w0_t[:, 1, :], w0_t[:, 2, :], w0_t[:, 3, :]),
            (w1_raw[:, 0, :], w_eff[:, 0, :], w_eff[:, 1, :], w1_raw[:, 3, :]))

    def max_loads(groups):
        return 16 * groups + 16 * max(0, groups - 2 * B)

    def pe_weights(pe, step):
        if step == 0:
            pe.wait_ge(wkv_ready, 1)
            pe.transpose(ps_alt[:, 0:D], wkv[:, :], ident[:, :])
            pe.transpose(ps_alt[:, D:2 * D], ffn0_raw[:, 0, :], ident[:, :])
            mm = pe.matmul(ps_alt[0:1, 2 * D:3 * D], bias0_cols[:, 2:3], w0_t[:, 3, :], start=True, stop=True)
        elif step == 1:
            pe.wait_ge(wp_sb, 1)
            pe.matmul(ps_acc[0:32, 0:D], down_raw[:, :], wt2[:, 0, :], start=True, stop=True)
            pe.matmul(ps_acc[:, D:2 * D], ffn0_raw[:, 1, :], wt2[:, 1, :], start=True, stop=True)
            pe.wait_ge(brow_ready, 1)
            mm = pe.matmul(ps_acc[:, 2 * D:3 * D], ones_row[:, :], bias_row[:, :], start=True, stop=True)
        else:
            pe.wait_ge(wp_sb, 2)
            pe.matmul(ps_alt[:, 0:D], down_t[:, :], up_raw[:, 0, :], start=True, stop=True)
            pe.matmul(ps_alt[:, D:2 * D], down_t[:, :], up_raw[:, 1, :], start=True, stop=True)
            mm = pe.matmul(ps_alt[:, 2 * D:3 * D], wa_t[:, :], ffn0_raw[:, 2, :], start=True, stop=True)
        mm.then_inc(wp_ps, 1)

    def act_weights(act, step):
        act.wait_ge(wp_ps, step + 1)
        if step == 0:
            cp = act.activation(wt2[:, :, :].rearrange("p n d -> p (n d)"), ps_alt[:, 0:2 * D], ACT.Copy)
        elif step == 1:
            act.activation(down_t[:, :], ps_acc[0:32, 0:D], ACT.Copy)
            act.activation(wa_t[:, :], ps_acc[:, D:2 * D], ACT.Copy)
            cp = act.activation(bias_bc[:, :], ps_acc[:, 2 * D:3 * D], ACT.Copy)
        else:
            cp = act.activation(w_eff[:, :, :].rearrange("p n d -> p (n d)"), ps_alt[:, 0:3 * D], ACT.Copy)
        cp.then_inc(wp_sb, 1)

    last_reader = {}

    def bank_free(pe, bank_index):
        if bank_index in last_reader:
            pe.wait_ge(*last_reader[bank_index])

    def logits_bank(it, s):
        return ps_main[s % 2] if layer_of(it) else (*ps_main, ps_alt)[(16 * it + s) % 3]

    def pe_scores(pe, it, s):
        h, par = ORDER[s], it % 2
        if s % HALF == 0:
            pe.wait_ge(ld_l[par][s // HALF], 48 * (it // 2 + 1))
        need(pe, max_ready, 16 * it + s - 1)
        for t in range(QT):
            mm = pe.matmul(ps_score[s % 2][:, t * T:(t + 1) * T], stack[0:K_SCORE, par, 0, h, t * P:(t + 1) * P],
                           stack[0:K_SCORE, par, 1, h, :], start=True, stop=True)
        mm.then_inc(score_ps, 1)

    def pe_logits(pe, it, s):
        h, par = ORDER[s], it % 2
        c = 16 * it + s
        if s % HALF == 0:
            pe.wait_ge(max_loaded, max_loads(2 * it + s // HALF + 1))
            if layer_of(it):
                pe.wait_ge(ld_u[par][s // HALF], 48 * ((it - B) // 2 + 1))
        need(pe, probs_ready, c - (1 if layer_of(it) else 2))
        main = logits_bank(it, s)

        def key(v, rows, t):
            return stack[0:rows, par, v, h, t * P:(t + 1) * P]

        def query(v, rows, lo, hi):
            return stack[0:rows, par, v, h, lo:hi]

        if layer_of(it) == 0:
            if c == 0:
                pe.wait_ge(pos_loaded, 64)
                pe.wait_ge(al_id_ready, 1)
            for t in range(QT):
                o = 1 - t
                d0, f0 = t * T + t * P, t * T + o * P
                pe.matmul(main[:, d0:d0 + P], key(1, K_DIAG, t), query(0, K_DIAG, t * P, t * P + P), start=True,
                          stop=added(s))
                if not added(s):
                    pe.matmul(main[:, d0:d0 + P], dist16[:, :], al_id[:, 0, h, :], start=False, stop=False)
                    pe.matmul(main[:, d0:d0 + P], dist16[:, :], al_id[:, 1, h, :], start=False, stop=True)
                mm = pe.matmul(main[:, f0:f0 + P], key(1, K_OFF, t), query(0, K_OFF, o * P, o * P + P), start=True, stop=True)
        else:
            pe.matmul(main[:, 0:T], key(1, K_DIAG, 0), query(0, K_DIAG, 0, T), start=True, stop=True)
            pe.matmul(main[:, T:2 * T], key(3, K_DIAG, 1), query(2, K_DIAG, 0, T), start=True, stop=True)
            need(pe, chosen, c - 16 * B)
            pe.matmul(ps_alt[:, 0:P], key(3, K_DIAG, 0), query(2, K_DIAG, 0, P), start=True, stop=True)
            mm = pe.matmul(ps_alt[:, P:2 * P], key(1, K_DIAG, 1), query(0, K_DIAG, P, T), start=True, stop=True)
        mm.then_inc(logits_ps, 1)

    def pe_pv(pe, it, g, t):
        need(pe, probs_ready, 16 * it + 4 * g + 4)
        if g == 0:
            need(pe, acc_ready, it)
            pe.wait_ge(v_sb, it + 1)
        r, e = g // 2, g % 2
        for j in range(4):
            mm = pe.matmul(ps_acc[32 * j:32 * j + 32, r * T:(r + 1) * T],
                           vpad[:, it % 2, t, HALF * r + 2 * j + e, :], probs[:, (4 * g + j) % RING, t, :],
                           start=(e == 0 and t == 0), stop=(e == 1 and t == 1))
        if t == QT - 1:
            mm.then_inc(pv_done, 1)

    def pe_max_t(pe, it, half):
        b = bank_of("max", it)
        pe.wait_ge(max_ready, 16 * it + 8 * half + 8)
        bank_free(pe, b)
        pe.transpose(bank[b][0:16, 0:P], mx[:, 16 * half:16 * half + 16], ident[:, :]).then_inc(maxt_ps, 1)
        last_reader[b] = (maxt_sb, 2 * it + half + 1)

    def pe_transpose_pair(pe, b, src):
        for t in range(QT):
            mm = pe.transpose(bank[b][:, t * P:(t + 1) * P], src[:, t, :], ident[:, :])
        return mm

    def pe_hidden(pe, it, g, tiles):
        b = bank_of(f"h{g}", it)
        n1 = it - B
        if tiles[0] == 0:
            if g == 0:
                pe.wait_ge(f_lo, n1 + 1)
            if g == 2:
                pe.wait_ge(h_lo, 4 * n1 + 2)
            bank_free(pe, b)
        for j in tiles:
            k0 = (2 * (g % 2) + j) * P
            terms = [(w_ff0[:, k0:k0 + P], fx16[:, p, :]) for p in range(2)] if g < 2 else \
                    [(w_ff1[:, k, k0:k0 + P], fh[:, 0, p, k, :]) for k in range(4) for p in range(2)]
            for n, (w, v) in enumerate(terms):
                mm = pe.matmul(bank[b][:, j * T:(j + 1) * T], w, v, start=(n == 0), stop=(n == len(terms) - 1))
        if tiles[-1] == 1:
            mm.then_inc(h_ps, 1)
            last_reader[b] = (h_sb, 4 * n1 + g + 1)

    def pe_qk(pe, it):
        b = bank_of("qk", it)
        pe.wait_ge(xnt_sb, it + 1)
        bank_free(pe, b)
        for w in range(2):
            mm = pe.matmul(bank[b][:, w * T:(w + 1) * T], proj[layer_of(it)][w], xn_t[:, it % 2, :],
                           start=True, stop=True)
        mm.then_inc(qk_ps, 1)
        last_reader[b] = (qk_out, it + 1)

    def pe_token_product(pe, b, lhs_t, weight):
        for t in range(QT):
            mm = pe.matmul(bank[b][:, t * D:(t + 1) * D], lhs_t[:, t * P:(t + 1) * P], weight, start=True, stop=True)
        return mm

    def pe_v(pe, it):
        b = bank_of("v", it)
        bank_free(pe, b)
        pe_token_product(pe, b, xn_t[:, it % 2, :], proj[layer_of(it)][2]).then_inc(v_ps, 1)
        last_reader[b] = (v_sb, it + 1)

    def pe_acc_t(pe, it):
        b = bank_of("acc", it)
        pe.wait_ge(acc_ready, it + 1)
        bank_free(pe, b)
        for blk in range(4):
            mm = pe.transpose(bank[b][:, blk * P:(blk + 1) * P], acc_sb[:, blk * P:(blk + 1) * P], ident[:, :])
        mm.then_inc(acct_ps, 1)
        last_reader[b] = (att_ready, it + 1)

    def pe_att_t(pe, it):
        b = bank_of("att", it)
        pe.wait_ge(att_ready, it + 1)
        bank_free(pe, b)
        pe_transpose_pair(pe, b, att).then_inc(attt_ps, 1)
        last_reader[b] = (attt_sb, it + 1)

    def pe_proj(pe, it):
        b = bank_of("proj", it)
        pe.wait_ge(attt_sb, it + 1)
        bank_free(pe, b)
        pe_token_product(pe, b, att_t, proj[layer_of(it)][3]).then_inc(proj_ps, 1)
        last_reader[b] = (x_attended, it + 1)

    def pe_ft(pe, it):
        b = bank_of("ft", it)
        pe.wait_ge(f_xn, it + 1)
        bank_free(pe, b)
        pe_transpose_pair(pe, b, fxn).then_inc(ft_ps, 1)
        last_reader[b] = (ft_sb, it + 1)

    def pe_f0(pe, it):
        b = bank_of("f0", it)
        pe.wait_ge(ft_sb, it + 1)
        bank_free(pe, b)
        for t in range(QT):
            out = bank[b][:, t * D:(t + 1) * D]
            pe.matmul(out, fxn_t[:, t * P:(t + 1) * P], w_eff[:, 2, :], start=True, stop=False)
            mm = pe.matmul(out, ones_row[:, :], bf_row[:, :], start=False, stop=True)
        mm.then_inc(f0_ps, 1)
        last_reader[b] = (f0_tanh, it + 1)

    def pe_out(pe, it):
        b = bank_of("out", it)
        pe.wait_ge(h_lo, 4 * (it - B + 1))
        bank_free(pe, b)
        for t in range(QT):
            for n, (k, p) in enumerate([(k, p) for k in range(4) for p in range(2)]):
                mm = pe.matmul(bank[b][:, t * D:(t + 1) * D], fh[:, 1, p, k, t * P:(t + 1) * P],
                               w_ff2[:, k, :], start=(n == 0), stop=(n == 7))
        mm.then_inc(h2_ps, 1)
        last_reader[b] = (out_ready, it - B + 1)

    def pe_xn_t(pe, it):
        b = bank_of("xn", it)
        pe.wait_ge(ln_xn, it + 1)
        bank_free(pe, b)
        pe_transpose_pair(pe, b, xn).then_inc(xnt_ps, 1)
        last_reader[b] = (xnt_sb, it + 1)

    def pe_iteration(pe, i):
        a0, f, late = i - 2, i - 3, i - 4
        for s in range(H):
            if i == 0 and s == 0:
                pe_qk(pe, 1)
            if has1(i - 1):
                pe_logits(pe, i - 1, s)
            if has(i):
                pe_scores(pe, i, s)
            if has0(i - 1):
                pe_logits(pe, i - 1, s)
            if has(i - 1) and s == 0:
                pe_max_t(pe, i - 1, 1)
            if s == 0 and has1(late):
                pe_hidden(pe, late, 2, [1])
            if s % 4 in (2, 3) and s > 3 and has(i - 1):
                pe_pv(pe, i - 1, s // 4 - 1, s % 4 - 2)
            if s in (2, 3) and has(a0):
                pe_pv(pe, a0, 3, s - 2)
            if s == at("qk", i) and has(i + 1) and i != 0:
                pe_qk(pe, i + 1)
            if s == at("v", i) and has(i):
                pe_v(pe, i)
            if s == at("ft", i) and has(f):
                pe_ft(pe, f)
            if s in (4, 5) and has1(late):
                pe_hidden(pe, late, 3, [s - 4])
            if s == at("acc", i) and has(a0):
                pe_acc_t(pe, a0)
            if s == at("f0", i) and has0(f):
                pe_f0(pe, f)
            for g in range(2):
                if s == at(f"h{g}", i) and has1(f):
                    pe_hidden(pe, f, g, [0, 1])
            if s == (at("max", i) if i else 8) and has(i):
                pe_max_t(pe, i, 0)
            if s == at("out", i) and has1(late):
                pe_out(pe, late)
            if s == at("att", i) and has(a0):
                pe_att_t(pe, a0)
            if s == at("proj", i) and has(a0):
                pe_proj(pe, a0)
            if s == at("xn", i) and has(i + 2):
                pe_xn_t(pe, i + 2)
            if s == 15 and has1(f):
                pe_hidden(pe, f, 2, [0])
            if i == 0 and s in (4, 6, 8):
                pe_weights(pe, s // 2 - 2)

    def pe_end(pe):
        a, b, c = ITEMS - 3, ITEMS - 2, ITEMS - 1
        pe_pv(pe, c, 3, 0)
        pe_pv(pe, c, 3, 1)
        pe_hidden(pe, a, 2, [1])
        pe_acc_t(pe, c)
        pe_hidden(pe, a, 3, [0])
        pe_ft(pe, b)
        pe_att_t(pe, c)
        pe_hidden(pe, a, 3, [1])
        pe_proj(pe, c)
        pe_hidden(pe, b, 0, [0, 1])
        pe_hidden(pe, b, 1, [0, 1])
        pe_out(pe, a)
        pe_hidden(pe, b, 2, [0, 1])
        pe_ft(pe, c)
        pe_hidden(pe, b, 3, [0, 1])
        pe_hidden(pe, c, 0, [0, 1])
        pe_hidden(pe, c, 1, [0, 1])
        pe_out(pe, b)
        pe_hidden(pe, c, 2, [0, 1])
        pe_hidden(pe, c, 3, [0, 1])
        pe_out(pe, c)

    def dve_stats(dve, it, x, st, semaphore, tiles=range(QT)):
        for t in tiles:
            dve.bn_stats(st[:, t, :], x[:, t, :]).then_inc(semaphore, 1)

    def dve_mean(dve, it, st, m, semaphore):
        dve.wait_ge(semaphore, 4 * it + 2)
        for t in range(QT):
            dve.bn_aggr(m[:, t, :], st[:, t, :]).then_inc(semaphore, 1)

    def dve_choose(dve, it, s):
        dve.wait_ge(logits_ps, 16 * it + s + 1)
        diag = logits_bank(it, s)[:, :].rearrange("p (a c) -> p a c", a=4)[:, 0:4:3, :]
        dve.copy_predicated(diag, masks[:, :, :].bitcast(U32),
                            ps_alt[:, 0:2 * P].rearrange("p (a c) -> p a c", a=2)).then_inc(chosen, 1)

    def dve_add(dve, it, s):
        dve.wait_ge(logits_ps, 16 * it + s + 1)
        diag = logits_bank(it, s)[:, :].rearrange("p (a c) -> p a c", a=4)[:, 0:4:3, :]
        dve.tensor_tensor(diag, diag, adist[:, ORDER[s], P:2 * P].unsqueeze(1).to_broadcast([P, 2, P]),
                          ALU.add).then_inc(dist_added, 1)

    def dve_max(dve, it, s):
        h = ORDER[s]
        dve.wait_ge(score_ps, 16 * it + s + 1)
        if s % HALF == 0:
            need(dve, maxt_ps, 2 * it - 1 + s // HALF)
        one = layer_of(it) == 1
        tab = ratio[:, :] if one else adist[:, h, :]
        for t in range(QT):
            dve.tensor_tensor_reduce(
                red_out[:, (2 * s + t) % 4, :], ps_score[s % 2][:, t * T:(t + 1) * T],
                tab[:, (1 - t) * P:(1 - t) * P + T], 1.0, NEG_BIG, ALU.mult if one else ALU.add, ALU.max,
                mx[:, 2 * h + t:2 * h + t + 1]).then_inc(max_ready if t == 1 else red_first, 1)

    def dve_hi(dve, n, form):
        if layer_of(n) == 0:
            dve.wait_ge(qk_out, n + 1)
        else:
            dve.wait_ge(xf_scaled, 2 * (n - B) + form + 1)
        if form == 0:
            need(dve, bounced, 64 * pairs(n))
        v = 2 * form
        dve.tensor_copy(parts[:, 0, v:v + 2, :], xf[:, v:v + 2, :]).then_inc(hi_ready, 1)

    def dve_attention(dve, m, steps):
        acc = bank[bank_of("acc", m)][:, :]
        for step in steps:
            if step == 0:
                dve.wait_ge(acct_ps, m + 1)
                den = acc.rearrange("p (b j c) -> p b j c", b=4, c=16)
                dve.reciprocal(rden[:, :, :], den[:, :, :, HD]).then_inc(rden_ready, 1)
                continue
            if step == 1:
                dve.wait_ge(rden_ready, m + 1)
                need(dve, attt_ps, m)
            t = step - 1
            num = acc.rearrange("p (r t j c) -> p t r j c", r=2, t=2, c=16)[:, t, :, :, 0:HD]
            rd = rden[:, t:4:2, :].unsqueeze(3).to_broadcast([P, 2, 8, HD])
            tt = dve.tensor_tensor(att[:, t, :].rearrange("p (r j c) -> p r j c", r=2, c=HD), num, rd, ALU.mult)
            if step == 2:
                tt.then_inc(att_ready, 1)

    def dve_residual(dve, m):
        dve.wait_ge(proj_ps, m + 1)
        if layer_of(m) == 0:
            dve.wait_ge(x_biased, m + 1)
        dve.tensor_tensor(x_item(m), bank[bank_of("proj", m)][:, 0:T].rearrange("p (t d) -> p t d", t=QT), x_item(m),
                          ALU.add).then_inc(x_attended, 1)

    def dve_f_stats(dve, m, tiles):
        dve.wait_ge(x_attended, m + 1)
        dve_stats(dve, m, x_item(m), fstats, f_stats, tiles)

    def dve_f_mean(dve, f):
        need(dve, f_xn, f)
        dve_mean(dve, f, fstats, fmv, f_stats)

    def dve_out(dve, it):
        b = it - B
        dve.wait_ge(h2_ps, b + 1)
        if b >= 2:
            dve.wait_ge(out_stored[b % 2], 16 * (b // 2))
        dve.scalar_tensor_tensor(out=outb[:, b % 2, :], in0=bank[bank_of("out", it)][:, 0:T], scalar=s_cols[:, 2:3],
                                 in1=x_item(b).rearrange("p t d -> p (t d)"),
                                 op0=ALU.mult, op1=ALU.add).then_inc(out_ready, 1)

    def dve_iteration(dve, i):
        n = i + 2
        for s in range(H):
            if i == 0 and s == 0:
                dve_hi(dve, 1, 0)
            if has1(i - 1):
                dve_choose(dve, i - 1, s)
            if has0(i - 1) and s > 0 and added(s - 1):
                dve_add(dve, i - 1, s - 1)
            if has(i):
                dve_max(dve, i, s)
            if has0(i - 1) and s == H - 1 and added(s):
                dve_add(dve, i - 1, s)
            if s == at("stats0", i) and has(n):
                if n == 0:
                    dve.wait_ge(ld_x0, 16)
                elif n == 1:
                    dve.wait_ge(ld_x, 16)
                elif layer_of(n) == 1:
                    dve.wait_ge(x_ffn0, n - B + 1)
            for t in range(QT):
                if s == at(f"stats{t}", i) and has(n):
                    dve_stats(dve, n, x_item(n), stats, ln_stats, [t])
            if s == at("mean", i) and has(n):
                need(dve, ln_xn, n)
                dve_mean(dve, n, stats, mv, ln_stats)
            if s == at("hi0", i) and has(i + 1) and i != 0:
                dve_hi(dve, i + 1, 0)
            if s == at("hi1", i) and has1(i + 1):
                dve_hi(dve, i + 1, 1)
            for step in range(3):
                if s == at(f"acc_out{step}", i) and has(i - 2):
                    dve_attention(dve, i - 2, [step])
            if s == at("out_out", i) and has1(i - 4):
                dve_out(dve, i - 4)
            if s == at("proj_out", i) and has(i - 2):
                dve_residual(dve, i - 2)
            for t in range(QT):
                if s == at(f"f_stats{t}", i) and has(i - 2):
                    dve_f_stats(dve, i - 2, [t])
            if s == at("f_mean", i) and has(i - 2):
                dve_f_mean(dve, i - 2)
            if i == 0 and s == 5:
                dve.wait_ge(ld_bias, 32)
                dve.wait_ge(wp_sb, 1)
                dve.tensor_tensor(bias_row[:, :], ps_alt[0:1, 2 * D:3 * D], bo_row[:, :], ALU.add).then_inc(brow_ready, 1)

    def dve_end(dve):
        a, b, c = ITEMS - 3, ITEMS - 2, ITEMS - 1
        dve_attention(dve, c, [0, 1, 2])
        low_input(dve, b)
        dve_residual(dve, c)
        dve_f_stats(dve, c, [0, 1])
        dve_f_mean(dve, c)
        low_hidden(dve, b, 0)
        low_hidden(dve, b, 1)
        dve_out(dve, a)
        low_input(dve, c)
        low_hidden(dve, b, 2)
        low_hidden(dve, b, 3)
        low_hidden(dve, c, 0)
        low_hidden(dve, c, 1)
        dve_out(dve, b)
        low_hidden(dve, c, 2)
        low_hidden(dve, c, 3)
        dve_out(dve, c)

    def max_store(eng, it, half):
        eng.wait_ge(maxt_sb, 2 * it + half + 1)
        need(eng, max_loaded, max_loads(2 * it + half + 1 - 4))
        eng.dma_start(dmax[it % 2][half].rearrange("h (t q) -> (h t) q", t=QT), negmax[:, half, :]).then_inc(max_stored, 16)

    def max_load(eng, it, half):
        eng.wait_ge(max_stored, 16 * (2 * it + half + 1))
        for v in range(1 + layer_of(it)):
            eng.dma_start(stack[ROW_MAX:ROW_MAX + 1, it % 2, 2 * v, HALF * half:HALF * (half + 1), :],
                          dmax[it % 2][half:half + 1]).then_inc(max_loaded, 16)

    def act_max(act, it, half):
        act.wait_ge(maxt_ps, 2 * it + half + 1)
        need(act, max_stored, 16 * (2 * it + half - 1))
        act.activation(negmax[:, half, :], bank[bank_of("max", it)][0:16, 0:P], ACT.Copy, scale=-1.0).then_inc(maxt_sb, 1)

    def act_hidden(act, it, g):
        n = 4 * (it - B) + g
        act.wait_ge(h_ps, n + 1)
        if g == 0:
            act.wait_ge(s2_ready, 1)
        need(act, h_lo, n - 1)
        if g in (0, 1):
            need(act, h_ps, 4 * (it - B))
        else:
            need(act, h2_ps, it - B)
        l, b = g // 2, bank_of(f"h{g}", it)
        act.activation(fh[:, l, 0, 2 * (g % 2):2 * (g % 2) + 2, :], bank[b][:, :].rearrange("p (k c) -> p k c", k=2),
                       ACT.Relu, scale=s2_cols[:, l:l + 1])
        act.activation(fr[:, g % 2, :], bank[b][:, :], ACT.Relu, scale=s2_cols[:, l:l + 1]).then_inc(h_sb, 1)

    def act_exp(act, it, s):
        c = 16 * it + s
        if layer_of(it) == 1:
            act.wait_ge(chosen, c - 16 * B + 1)
        elif added(s):
            act.wait_ge(dist_added, added_before(c + 1))
        else:
            act.wait_ge(logits_ps, c + 1)
        if s % 4 == 0:
            need(act, pv_done, c // 4 - 1)
        act.activation(probs[:, s % RING, :, :], logits_bank(it, s)[:, :].rearrange("p (a c) -> p a c", a=2),
                       ACT.Exp).then_inc(probs_ready, 1)

    def act_qk(act, n):
        ps = bank[bank_of("qk", n)]
        act.wait_ge(qk_ps, n + 1)
        if layer_of(n) == 0:
            if n == 0:
                act.wait_ge(bq_ready, 1)
            need(act, lo_ready, n)
            act.activation(xf[:, 0, :], ps[:, 0:T], ACT.Identity, bias=bq_s[:, 0:1], scale=SCALE[0])
            act.activation(xf[:, 1, :], ps[:, T:2 * T], ACT.Identity, bias=bq_s[:, 1:2]).then_inc(qk_out, 1)
        else:
            need(act, xf_scaled, 2 * (n - B))
            act.activation(qk_sb[:, :, :].rearrange("p a c -> p (a c)"), ps[:, :], ACT.Copy).then_inc(qk_out, 1)

    def act_v(act, it):
        act.wait_ge(v_ps, it + 1)
        need(act, pv_done, 4 * (it - 1))
        if it == 0:
            act.wait_ge(const_ready, 2)
        dst = vpad[:, it % 2, :, :, :].rearrange("p t (g e) (f c) -> p (t g) e f c", e=2, f=2)
        src = bank[bank_of("v", it)][:, 0:T].rearrange("p (g e c) -> p g e c", e=2, c=HD)
        for e in range(2):
            cp = act.activation(dst[:, :, e, e, 0:HD], src[:, :, e, :], ACT.Copy)
        cp.then_inc(v_sb, 1)

    def act_acc(act, m):
        act.wait_ge(pv_done, 4 * (m + 1))
        need(act, acct_ps, m)
        act.activation(acc_sb[:, :], ps_acc[:, :], ACT.Copy).then_inc(acc_ready, 1)

    def act_ft(act, f):
        ps = bank[bank_of("ft", f)]
        act.wait_ge(ft_ps, f + 1)
        if layer_of(f) == 0:
            need(act, f0_ps, f)
        else:
            need(act, f_lo, f - B)
            if f == B:
                act.wait_ge(f0_ps, B)
            need(act, h_ps, 4 * (f - B) - 2)
            act.activation(fx16[:, 0, :], ps[:, 0:T], ACT.Copy)
        act.activation(fxn_t[:, :], ps[:, 0:T], ACT.Copy).then_inc(ft_sb, 1)

    def act_att(act, m):
        act.wait_ge(attt_ps, m + 1)
        need(act, proj_ps, m)
        act.activation(att_t[:, :], bank[bank_of("att", m)][:, 0:T], ACT.Copy).then_inc(attt_sb, 1)

    def act_tanh(act, f):
        act.wait_ge(f0_ps, f + 1)
        need(act, x_ffn0, f)
        act.activation(fth[:, :], bank[bank_of("f0", f)][:, 0:T], ACT.Tanh).then_inc(f0_tanh, 1)

    def act_xn(act, n):
        act.wait_ge(xnt_ps, n + 1)
        need(act, v_ps, n - 1)
        act.activation(xn_t[:, n % 2, :], bank[bank_of("xn", n)][:, 0:T], ACT.Copy).then_inc(xnt_sb, 1)

    def act_norm_ffn(act, f):
        act_norm(act, f, fnegmean, frstd, fxn, f_rstd, f_xn, ft_ps)

    def act_norm(act, it, nm, r, out, r_sem, xn_sem, out_sem):
        act.wait_ge(r_sem, 3 * (it + 1))
        need(act, out_sem, it)
        for t in range(QT):
            cp = act.activation(out[:, t, :], x_item(it)[:, t, :], ACT.Identity, bias=nm[:, t:t + 1],
                                scale=r[:, t:t + 1])
        cp.then_inc(xn_sem, 1)

    def act_iteration(act, i):
        for s in range(H):
            if i == 0 and s == 0:
                act_qk(act, 1)
            if s == at("ft_out", i) and has1(i - 3):
                act_ft(act, i - 3)
            if has(i - 1):
                act_exp(act, i - 1, s)
            if s == 0 and has(i - 1):
                act_max(act, i - 1, 1)
                max_store(act, i - 1, 1)
            if s == at("h2_out", i) and has1(i - 4):
                act_hidden(act, i - 4, 2)
            if s == at("f_norm", i) and has(i - 3):
                act_norm_ffn(act, i - 3)
            if s == at("qk_out", i) and has(i + 1) and i != 0:
                act_qk(act, i + 1)
            if s == at("v_out", i) and has(i):
                act_v(act, i)
            if s == at("max_load1", i) and has(i - 1):
                max_load(act, i - 1, 1)
            if s == at("acc_out", i) and has(i - 2):
                act_acc(act, i - 2)
            if s == at("h3_out", i) and has1(i - 4):
                act_hidden(act, i - 4, 3)
            if s == at("ft_out", i) and has0(i - 3):
                act_ft(act, i - 3)
            if s == at("f0_out", i) and has0(i - 3):
                act_tanh(act, i - 3)
            if s == (at("max_out", i) if i else 8) and has(i):
                act_max(act, i, 0)
                max_store(act, i, 0)
            for g in range(2):
                if s == at(f"h{g}_out", i) and has1(i - 3):
                    act_hidden(act, i - 3, g)
            if s == at("att_out", i) and has(i - 2):
                act_att(act, i - 2)
            if s == at("norm", i) and has(i + 2):
                act_norm(act, i + 2, negmean, rstd, xn, ln_rstd, ln_xn, xnt_ps)
            if s == (at("max_load0", i) if i else 10) and has(i):
                max_load(act, i, 0)
            if s == at("xn_out", i) and has(i + 2):
                act_xn(act, i + 2)
            if i == 2 and s in (7, 9, 11, 13, 15):
                act.wait_ge(toe_min_ready, 1)
                if s == 7:
                    act.activation(ratio[:, :], toe_min[:, :], ACT.Exp, scale=2 * LAMBDA)
                else:
                    v = (s - 9) // 2
                    ex = act.activation(rowscale[:, v, :], cen[:, :], ACT.Exp, scale=(-1, 1, 1, -1)[v] * LAMBDA)
                    if v == 3:
                        ex.then_inc(tab1_exp, 1)
            if i == 0:
                if s in (4, 6, 8):
                    act_weights(act, s // 2 - 2)
                if s == 0:
                    act.wait_ge(alf_ready, 1)
                    act.wait_ge(id_ready, 2)
                for p in range(2):
                    h = ORDER[s]
                    cp = act.activation(al_id[:, p, h, :], ident[:, :], ACT.Copy, scale=alf[:, p, h:h + 1])
                if s == H - 1:
                    cp.then_inc(al_id_ready, 1)

    def act_end(act):
        a, b, c = ITEMS - 3, ITEMS - 2, ITEMS - 1
        act_acc(act, c)
        act_norm_ffn(act, b)
        act_hidden(act, a, 2)
        act_ft(act, b)
        act_att(act, c)
        act_hidden(act, a, 3)
        act_hidden(act, b, 0)
        act_hidden(act, b, 1)
        act_norm_ffn(act, c)
        act_ft(act, c)
        act_hidden(act, b, 2)
        act_hidden(act, b, 3)
        act_hidden(act, c, 0)
        act_hidden(act, c, 1)
        act_hidden(act, c, 2)
        act_hidden(act, c, 3)

    def pool_norm(pool, it, m, v, nm, r, st_sem, r_sem, xn_sem):
        pool.wait_ge(st_sem, 4 * (it + 1))
        need(pool, xn_sem, it)
        pool.tensor_tensor(v[:, QT:2 * QT], m[:, :, 0], minus1[:, :], ALU.mult)
        pool.tensor_tensor(v[:, 0:QT], m[:, :, 1], eps_c[:, :], ALU.add).then_inc(r_sem, 1)
        pool.wait_ge(r_sem, 3 * it + 1)
        pool.tensor_tensor(r[:, :], v[:, 0:QT], mhalf[:, :], ALU.pow).then_inc(r_sem, 1)
        pool.wait_ge(r_sem, 3 * it + 2)
        pool.tensor_tensor(nm[:, :], v[:, QT:2 * QT], r[:, :], ALU.mult).then_inc(r_sem, 1)

    def pool_low(pool, k, v):
        pool.wait_ge(hi_ready, k + 1)
        pool.tensor_tensor(parts[:, 1, v:v + 2, :], xf[:, v:v + 2, :], parts[:, 0, v:v + 2, :],
                           ALU.subtract).then_inc(lo_ready, 1)

    def pool_scale(pool, n, form):
        if form == 0:
            pool.wait_ge(qk_out, n + 1)
            if n == B:
                pool.wait_ge(tab1_ready, 1)
                pool.wait_ge(lo_ready, B)
        pool.tensor_tensor(xf[:, 2 * form:2 * form + 2, :], qk_sb[:, :, :], rowscale[:, 2 * form:2 * form + 2, :],
                           ALU.mult).then_inc(xf_scaled, 1)

    def low_input(eng, f):
        eng.wait_ge(ft_sb, f + 1)
        eng.tensor_tensor(fx16[:, 1, :], fxn_t[:, :], fx16[:, 0, :], ALU.subtract).then_inc(f_lo, 1)

    def low_hidden(eng, it, g):
        n = 4 * (it - B) + g
        eng.wait_ge(h_sb, n + 1)
        need(eng, h_lo, n)
        l, k = g // 2, 2 * (g % 2)
        eng.tensor_tensor(fh[:, l, 1, k:k + 2, :], fr[:, g % 2, :].rearrange("p (k c) -> p k c", k=2),
                          fh[:, l, 0, k:k + 2, :], ALU.subtract).then_inc(h_lo, 1)

    def pool_norm_attention(pool, it):
        pool_norm(pool, it, mv, vpe, negmean, rstd, ln_stats, ln_rstd, ln_xn)

    def pool_bias(pool, it):
        if it == 0:
            pool.wait_ge(wp_sb, 2)
        pool.wait_ge(ln_xn, it + 1)
        pool.tensor_tensor(x_item(it), x_item(it), bias_bc[:, :].unsqueeze(1).to_broadcast([P, QT, D]),
                           ALU.add).then_inc(x_biased, 1)

    def pool_iteration(pool, i):
        f, n = i - 3, i + 1
        if has(f):
            pool_norm_ffn(pool, f)
        if has(i - 4) and layer_of(i - 4) == 1:
            low_hidden(pool, i - 4, 2)
        if has(n):
            if layer_of(n) == 1:
                pool_scale(pool, n, 0)
                pool_scale(pool, n, 1)
            pool_low(pool, pairs(n), 0)
        if has(f) and layer_of(f) == 1:
            low_input(pool, f)
        if has(i - 4) and layer_of(i - 4) == 1:
            low_hidden(pool, i - 4, 3)
        if has(n) and layer_of(n) == 1:
            pool_low(pool, pairs(n) + 1, 2)
        if has(i + 2):
            pool_norm_attention(pool, i + 2)
        if has(f) and layer_of(f) == 0:
            pool.wait_ge(f0_tanh, f + 1)
            pool.tensor_tensor(x_item(f), x_item(f), fth[:, :].rearrange("p (t d) -> p t d", t=QT),
                               ALU.add).then_inc(x_ffn0, 1)
        if has(f) and layer_of(f) == 1:
            low_hidden(pool, f, 0)
        if has(f) and layer_of(f) == 1:
            low_hidden(pool, f, 1)
        if i == 0:
            pool_bias(pool, 0)
            pool_bias(pool, 1)
        if 2 <= i + 2 < B:
            pool_bias(pool, i + 2)

    def pool_norm_ffn(pool, f):
        pool_norm(pool, f, fmv, fvpe, fnegmean, frstd, f_stats, f_rstd, f_xn)

    def pool_end(pool):
        a, b, c = ITEMS - 3, ITEMS - 2, ITEMS - 1
        pool_norm_ffn(pool, b)
        low_hidden(pool, a, 2)
        low_hidden(pool, a, 3)
        pool_norm_ffn(pool, c)

    def sp_bounce(sp, n, form):
        k = pairs(n) + form
        sp.wait_ge(lo_ready, k + 1)
        par = n % 2
        for half in range(2):
            need(sp, (ld_u if form else ld_l)[par][half], 48 * ((n - B if form else n) // 2))
        for v in (2 * form, 2 * form + 1):
            for p in range(2):
                sp.dma_start(dqk[par][v, p].rearrange("d h t -> h d t"), parts[:, p, v, :]).then_inc(bounced, 16)
        sp.wait_ge(bounced, 64 * (k + 1))

    def sp_stack(sp, n, form, half):
        par = n % 2
        hs = slice(HALF * half, HALF * (half + 1))
        done = (ld_u if form else ld_l)[par][half]
        need(sp, logits_ps, 16 * (n - 2) + 8 * (half + 1))
        if form == 1 and n == B:
            sp.wait_ge(stack_clear, 6)
        q, k = dqk[par][2 * form], dqk[par][2 * form + 1]
        sp.dma_start(stack[0:2 * PART_ROWS, par, 2 * form, hs, :],
                     q[:, :, hs, :].rearrange("p d h t -> (p d) (h t)").unsqueeze(0)
                     .to_broadcast([2, PART_ROWS, HALF * T])).then_inc(done, 16)
        for p in range(2):
            sp.dma_start(stack[PART_ROWS * p:PART_ROWS * (p + 1), par, 2 * form + 1, hs, :],
                         k[p, :, hs, :].rearrange("d h t -> d (h t)").unsqueeze(0)
                         .to_broadcast([2, HD, HALF * T])).then_inc(done, 16)

    def sp_out(sp, it):
        b = it - B
        sp.wait_ge(out_ready, b + 1)
        sp.dma_start(out_d[:, b * QT:(b + 1) * QT, :],
                     outb[:, b % 2, :].rearrange("p (t d) -> p t d", t=QT)).then_inc(out_stored[b % 2], 16)

    def sp_iteration(sp, i):
        n = i + 1
        if has(n):
            sp_bounce(sp, n, 0)
            if n < 2:
                sp.wait_ge(stack_clear, n + 1)
            sp_stack(sp, n, 0, 0)
            if layer_of(n) == 1:
                sp_bounce(sp, n, 1)
                sp_stack(sp, n, 1, 0)
        if has1(i - 4):
            sp_out(sp, i - 4)
        if has(n):
            sp_stack(sp, n, 0, 1)
            if layer_of(n) == 1:
                sp_stack(sp, n, 1, 1)

    def has(item):
        return 0 <= item < ITEMS

    def late_phase(i):
        return has1(i - 1)

    def at(step, i):
        return SLOTS[step][late_phase(i)]

    def has0(item):
        return has(item) and layer_of(item) == 0

    def has1(item):
        return has(item) and layer_of(item) == 1

    LAST = ITEMS + 1

    block = ctx.enter_context(nc.Block())

    @block.sync
    def _(sp):
        sp.dma_start(x_sb[:, 0:QT, :], x_d[:, 0:QT, :]).then_inc(ld_x0, 16)
        sp.dma_start(w0_raw[:, 0:3, :], a["L0_attn_qkv_w"].rearrange("(n p) d -> p n d", p=P)).then_inc(ld_w0, 16)
        sp.dma_start(w0_raw[:, 3, :], a["L0_attn_out_w"]).then_inc(ld_w0, 16)
        sp.dma_start(bias0_rows[:, :], a["L0_attn_qkv_b"].rearrange("(n p) -> n p", p=P)).then_inc(ld_w0, 16)
        sp.wait_ge(al_zero, 1)
        sp.dma_start(al[:, 0:H], a["L0_attn_decay_alpha"].partition_broadcast(P)).then_inc(ld_alpha, 16)
        sp.dma_start(al[0:H, H:H + 1], a["L0_attn_decay_alpha"].rearrange("(h o) -> h o", o=1)).then_inc(ld_alpha, 16)
        sp.dma_start(x_sb[:, QT:, :], x_d[:, QT:, :]).then_inc(ld_x, 16)
        for n, name in enumerate(("L1_attn_W_q", "L1_attn_W_k", "L1_attn_W_v", "L1_attn_W_o")):
            sp.dma_start(w1_raw[:, n, :], a[name]).then_inc(ld_w1, 16)
        for n, name in enumerate(("L0_ffn_weight", "L0_ffn_aux_weight1", "L0_ffn_aux_weight2")):
            sp.dma_start(ffn0_raw[:, n, :], a[name]).then_inc(ld_w1, 16)
        sp.dma_start(down_raw[:, :], a["L1_attn_W_down_kv"]).then_inc(ld_w1, 16)
        sp.dma_start(up_raw[:, 0, :], a["L1_attn_W_up_k"]).then_inc(ld_w1, 16)
        sp.dma_start(up_raw[:, 1, :], a["L1_attn_W_up_v"]).then_inc(ld_w1, 16)
        def load_last_weights():
            for n in range(3):
                sp.dma_start(s_cols[:, n:n + 1], a[f"L1_ffn_s{n}"].partition_broadcast(P)).then_inc(ld_s, 16)
            for lo, hi, name in ((0, 2, "L1_ffn_k0"), (2, 6, "L1_ffn_k1")):
                sp.dma_start(bool_raw[:, lo * FEAT:hi * FEAT].rearrange("p (n f) -> p n f", f=FEAT),
                             a[name].rearrange("(n p) f -> p n f", p=P)).then_inc(ld_bool, 16)
            sp.dma_start(bool_raw[:, 6 * FEAT:6 * FEAT + 4 * D].rearrange("p (n f) -> p n f", n=4),
                         a["L1_ffn_k2"].rearrange("(n p) f -> p n f", p=P)).then_inc(ld_bool, 16)

        sp_iteration(sp, -2)
        sp_iteration(sp, -1)
        sp.wait_ge(pos_ready, 1)
        sp.dma_start(dpos.rearrange("n h t -> h n t"), upos16[:, :, :]).then_inc(pos_stored, 16)
        sp.wait_ge(pos_stored, 16)
        sp.wait_ge(stack_clear, 2)
        for par in range(2):
            sp.dma_start(stack[ROW_POS:ROW_POS + 2, par, 0, :, :], dpos).then_inc(pos_loaded, 16)
            sp.dma_start(stack[ROW_POS + 2:ROW_POS + 4, par, 1, :, :], dpos).then_inc(pos_loaded, 16)
        for i in range(LAST):
            sp_iteration(sp, i)
            if i == 1:
                load_last_weights()
        for it in range(ITEMS - 3, ITEMS):
            sp_out(sp, it)
        for p in range(2):
            sp.wait_ge(out_stored[p], 16 * B // 2)

    @block.gpsimd
    def _(pool):
        pool.memset(al[:, :], 0.0).then_inc(al_zero, 1)
        pool.memset(ident[:, :], 0.0).then_inc(id_ready, 1)
        pool.wait_ge(id_ready, 1)
        pool.affine_select(out=ident[:, :], in_=ident[:, :], compare_op=ALU.not_equal, fill=1.0, base=0,
                           pattern=[[-1, P]], channel_multiplier=1).then_inc(id_ready, 1)
        pool.iota(toe_i[:, :], [[-1, 3 * P]], base=P, channel_multiplier=1).then_inc(iota_ready, 1)
        pool.iota(cen_i[:, :], [[1, T]], base=-P, channel_multiplier=0).then_inc(iota_ready, 1)
        pool.memset(eps_c[:, :], EPS)
        pool.memset(mhalf[:, :], -0.5)
        pool.memset(minus1[:, :], -1.0)
        pool.memset(ones_row[:, :], 1.0).then_inc(const_ready, 1)
        pool.wait_ge(const_ready, 1)
        pool_norm_attention(pool, 0)

        def clear(par, v, value):
            return pool.memset(stack[:, par, v, :, :].rearrange("p h t -> p (h t)").bitcast(U32), value)

        def clear_l(par):
            clear(par, 0, 0).then_inc(stack_zero, 1)
            pool.wait_ge(stack_zero, par + 1)
            pool.memset(stack[ROW_MAX:P, par, 0, :, :].rearrange("p h t -> p (h t)").bitcast(U32),
                        ONE_ONE).then_inc(stack_ones, 1)
            pool.wait_ge(stack_ones, par + 1)
            clear(par, 1, ONE_ONE).then_inc(stack_clear, 1)

        clear_l(0)
        pool_norm_attention(pool, 1)
        pool_low(pool, 0, 0)
        pool.dma_start(bo_row[:, :], a["L0_attn_out_b"].rearrange("(o n) -> o n", o=1)).then_inc(ld_bias, 16)
        pool.dma_start(bf_row[:, :], a["L0_ffn_bias"].rearrange("(o n) -> o n", o=1)).then_inc(ld_bias, 16)
        pool.memset(vpad[:, :, :, :, :], 0.0).then_inc(vpad_zero, 1)
        pool.wait_ge(vpad_zero, 1)
        for e in range(2):
            ms = pool.memset(vpad[:, :, :, :, :].rearrange("p a t (g e) c -> p (a t g) e c", e=2)
                             [:, :, e, 16 * e + HD:16 * e + HD + 1], 1.0)
        ms.then_inc(const_ready, 1)
        clear_l(1)
        for i in range(LAST):
            pool_iteration(pool, i)
            if 2 <= i < 6:
                clear(i // 2 - 1, 2 + i % 2, ONE_ONE if i % 2 else 0).then_inc(stack_clear, 1)
        pool_end(pool)

    @block.vector
    def _(dve):
        done = [0]

        def step(ins):
            done[0] += 1
            ins.then_inc(dve_setup, 1)
            dve.wait_ge(dve_setup, done[0])

        dve_iteration(dve, -2)
        dve.wait_ge(ld_alpha, 32)
        step(dve.tensor_scalar(al_tmp[:, 0, :], al[:, :], -1.0, None, ALU.mult))
        dve.tensor_tensor(al_tmp[:, 1, :], al[:, :], al_tmp[:, 0, :], ALU.max).then_inc(al_abs, 1)
        dve.wait_ge(w0_sb, 1)
        dve.tensor_scalar(bq_s[:, 0:1], bias0_cols[:, 0:1], SCALE[0], None, ALU.mult)
        dve.tensor_copy(bq_s[:, 1:2], bias0_cols[:, 1:2]).then_inc(bq_ready, 1)
        dve.wait_ge(iota_ready, 2)
        dve.tensor_copy(toe[:, :], toe_i[:, :])
        step(dve.tensor_copy(cen[:, :], cen_i[:, :]))
        dve.tensor_scalar(toe_abs[:, :], toe[:, :], -1.0, None, ALU.mult)
        step(dve.tensor_scalar(upos[:, 0, :], cen[0:H, :], -1.0, None, ALU.mult))
        dve.tensor_tensor(toe_abs[:, :], toe[:, :], toe_abs[:, :], ALU.max)
        step(dve.tensor_tensor(upos[:, 1, :], cen[0:H, :], upos[:, 0, :], ALU.max))
        dve_iteration(dve, -1)
        dve.wait_ge(softplus, 2)
        step(dve.scalar_tensor_tensor(out=al_tmp[:, 0, :], in0=al[:, :], scalar=0.0, in1=al_tmp[:, 3, :],
                                      op0=ALU.max, op1=ALU.add))
        step(dve.tensor_scalar(al_tmp[:, 1, :], al_tmp[:, 0, :], -1.0, None, ALU.mult))
        for h in ORDER:
            ts = dve.tensor_scalar(adist[:, h, :], toe_abs[:, :], al_tmp[:, 1, h:h + 1], None, ALU.mult)
        ts.then_inc(adist_ready, 1)
        step(dve.tensor_scalar(upos[:, 2, :], upos[:, 1, :], al_tmp[0:H, 1, H:H + 1], None, ALU.mult))
        step(dve.tensor_copy(upos16[:, 0, :], upos[:, 2, :]))
        dve.tensor_tensor(upos16[:, 1, :], upos[:, 2, :], upos16[:, 0, :], ALU.subtract).then_inc(pos_ready, 1)
        dve.tensor_scalar(dist16[:, :], toe_abs[:, P:2 * P], -1.0, None, ALU.mult)
        step(dve.tensor_copy(al16[:, :], al_tmp[:, 0, 0:H]))
        step(dve.tensor_copy(alf[:, 0, :], al16[:, :]))
        dve.tensor_tensor(alf[:, 1, :], al_tmp[:, 0, 0:H], alf[:, 0, :], ALU.subtract).then_inc(alf_ready, 1)
        dve.tensor_scalar(toe_min[:, :], toe[:, :], 0.0, None, ALU.min).then_inc(toe_min_ready, 1)
        dve.wait_ge(ld_w1, 160)
        dve.tensor_tensor(wkv[:, :], w1_raw[:, 1, :], w1_raw[:, 2, :], ALU.add).then_inc(wkv_ready, 1)
        dve.wait_ge(adist_ready, 1)
        for i in range(LAST):
            dve_iteration(dve, i)
            if i == 0:
                dve.tensor_scalar(masks[:, 0, :], toe[:, P:2 * P], 0.0, None, ALU.is_gt)
                dve.tensor_scalar(masks[:, 1, :], toe[:, P:2 * P], 0.0, None, ALU.is_lt)
            if i == 3:
                dve.wait_ge(tab1_exp, 1)
                for v in (0, 2):
                    ts = dve.tensor_scalar(rowscale[:, v, :], rowscale[:, v, :], SCALE[1], None, ALU.mult)
                ts.then_inc(tab1_ready, 1)
                dve.wait_ge(ld_s, 48)
                dve.tensor_scalar(s2_cols[:, :], s_cols[:, :], 2.0, None, ALU.mult).then_inc(s2_ready, 1)
            if i == 4:
                dve.wait_ge(ld_bool, 48)
                dve.tensor_tensor(w_ff0[:, :], bool_raw[:, 0:FEAT], bool_raw[:, FEAT:2 * FEAT],
                                  ALU.subtract).then_inc(wff_ready, 1)
            if i == 5:
                dve.wait_ge(wff_ready, 1)
                dve.tensor_scalar(w_ff0[:, :], w_ff0[:, :], 2.0, None, ALU.mult).then_inc(wff_ready, 1)
                dve.tensor_scalar(w_ff2[:, :, :].rearrange("p n f -> p (n f)"),
                                  bool_raw[:, 6 * FEAT:6 * FEAT + 4 * D], 2.0, -1.0, ALU.mult,
                                  ALU.add).then_inc(wff_ready, 1)
            if 6 <= i < 10:
                k = i - 6
                dve.tensor_scalar(w_ff1[:, k, :], bool_raw[:, (2 + k) * FEAT:(3 + k) * FEAT], 2.0, -1.0,
                                  ALU.mult, ALU.add).then_inc(wff_ready, 1)
        dve_end(dve)

    @block.scalar
    def _(act):
        act.wait_ge(w0_ps, 1)
        act.activation(bias0_cols[:, :], bank[7][:, 0:3], ACT.Copy)
        act.activation(w0_t[:, :, :].rearrange("p n d -> p (n d)"), bank[6][:, :], ACT.Copy).then_inc(w0_sb, 1)
        act_iteration(act, -2)
        act.wait_ge(al_abs, 1)
        act.activation(al_tmp[:, 2, :], al_tmp[:, 1, :], ACT.Exp, scale=-1.0).then_inc(softplus, 1)
        act.wait_ge(softplus, 1)
        act.activation(al_tmp[:, 3, :], al_tmp[:, 2, :], ACT.Ln, bias=1.0).then_inc(softplus, 1)
        act_iteration(act, -1)
        for i in range(LAST):
            act_iteration(act, i)
        act_end(act)

    @block.tensor
    def _(pe):
        pe.wait_ge(ld_w0, 48)
        pe.wait_ge(id_ready, 2)
        for n in range(4):
            pe.transpose(bank[6][:, n * D:(n + 1) * D], w0_raw[:, n, :], ident[:, :])
        pe.transpose(bank[7][:, 0:3], bias0_rows[:, :], ident[0:3, 0:3]).then_inc(w0_ps, 1)
        last_reader[6] = last_reader[7] = (w0_sb, 1)
        pe_iteration(pe, -2)
        pe_iteration(pe, -1)
        for i in range(LAST):
            pe_iteration(pe, i)
            if i == 0:
                pe.wait_ge(wp_sb, 3)
                pe.wait_ge(ld_bias, 32)
            if i == B + 2:
                pe.wait_ge(wff_ready, 7)
        pe_end(pe)


_INS = ['L0_attn_x', 'L0_attn_qkv_w', 'L0_attn_qkv_b', 'L0_attn_out_w', 'L0_attn_out_b', 'L0_attn_decay_alpha',
        'L0_ffn_weight', 'L0_ffn_aux_weight1', 'L0_ffn_aux_weight2', 'L0_ffn_bias', 'L1_attn_W_q', 'L1_attn_W_k',
        'L1_attn_W_v', 'L1_attn_W_o', 'L1_attn_W_down_kv', 'L1_attn_W_up_k', 'L1_attn_W_up_v', 'L1_ffn_k0',
        'L1_ffn_k1', 'L1_ffn_k2', 'L1_ffn_s0', 'L1_ffn_s1', 'L1_ffn_s2']


def kernel(**inputs):
    import numpy as _np
    import concourse.bacc as _bacc
    from concourse import mybir as _mybir
    from concourse.bass_utils import run_bass_kernel_spmd as _run

    nc = _bacc.Bacc("TRN2", target_bir_lowering=False, num_devices=1)
    arrays, aps = {}, {}
    for name in _INS:
        v = _np.ascontiguousarray(inputs[name])
        if v.ndim == 0 or name.startswith("L1_ffn_s"):
            v = v.reshape(1)
        arrays[f"in_{name}_dram"] = v
        aps[name] = nc.dram_tensor(f"in_{name}_dram", v.shape, _mybir.dt.from_np(v.dtype), kind="ExternalInput").ap()
    aps["out"] = nc.dram_tensor("out_0_dram", (8, 256, 128), _mybir.dt.float32, kind="ExternalOutput").ap()
    build(nc, aps)
    r = _run(nc, [arrays], core_ids=[0])
    return r.results[0]["out_0_dram"]
```
